# Optimizing a Trainium2 kernel written in Bass

```python
import numpy as np
import jax
import jax.numpy as jnp

def _softmax(x, axis=-1):
    return jax.nn.softmax(x, axis=axis)

def _gelu(x):
    return jax.nn.gelu(x, approximate=True)

def _silu(x):
    return jax.nn.silu(x)

def _sigmoid(x):
    return jax.nn.sigmoid(x)

def _layernorm(x, axis=-1, eps=1e-05):
    m = jnp.mean(x, axis=axis, keepdims=True)
    v = jnp.var(x, axis=axis, keepdims=True)
    return (x - m) / jnp.sqrt(v + eps)

def _scatter_add(tgt, idx, src, axis=0):
    return tgt.at[idx].add(src)

def _segment_sum(src, seg, n):
    return jax.ops.segment_sum(src, seg, n)
kernel_name = 'mk_gnn_resnorm_d1_gnn_r32_d19efb'

def setup_inputs(seed: int=0):
    np.random.seed(seed)
    _w = jnp.asarray

    def _rec_inputs():
        import jax
        import jax.numpy as jnp
        _gk = jax.random.key(seed)
        x = -0.0003713 + 1 * jax.random.normal(jax.random.fold_in(_gk, 1), (50000, 128), jnp.float32)
        src = jax.random.randint(jax.random.fold_in(_gk, 2), (50000,), 0, 50000, jnp.int32)
        dst = jax.random.randint(jax.random.fold_in(_gk, 3), (50000,), 0, 50000, jnp.int32)
        _o = jnp.argsort(dst, stable=True)
        src = src[_o]
        dst = dst[_o]
        edge_weight = jax.random.uniform(jax.random.fold_in(_gk, 12), (50000,), jnp.float32, 0.0, 1)
        return (x, src, dst, edge_weight)
    x, src, dst, edge_weight = _rec_inputs()

    def _L0_gnn_setup():
        import jax, jax.numpy as jnp
        import numpy as np
        N = 3125
        E = 25000
        D = 128
        key = jax.random.key(seed)
        ks = jax.random.split(key, 12)
        s = lambda fan_in: 1.0 / np.sqrt(fan_in)
        return {'h': jax.random.normal(ks[0], (N, D), dtype=jnp.float32), 'w': jax.random.uniform(ks[1], (E,), dtype=jnp.float32), 'src': jax.random.randint(ks[2], (E,), 0, N, dtype=jnp.int32), 'dst': jax.random.randint(ks[3], (E,), 0, N, dtype=jnp.int32), 'W1': jax.random.uniform(ks[4], (2 * D + 1, D), jnp.float32, -s(2 * D + 1), s(2 * D + 1)), 'b1': jnp.zeros((D,), jnp.float32), 'W2': jax.random.uniform(ks[5], (D, D), jnp.float32, -s(D), s(D)), 'b2': jnp.zeros((D,), jnp.float32), 'U1': jax.random.uniform(ks[6], (2 * D, D), jnp.float32, -s(2 * D), s(2 * D)), 'c1': jnp.zeros((D,), jnp.float32), 'U2': jax.random.uniform(ks[7], (D, D), jnp.float32, -s(D), s(D)), 'c2': jnp.zeros((D,), jnp.float32)}
    _L0_gnn_all = _L0_gnn_setup()
    _L0_gnn_in = {k: v for k, v in _L0_gnn_all.items() if k in ('W1', 'b1', 'W2', 'b2', 'U1', 'c1', 'U2', 'c2')}
    del _L0_gnn_all
    return {'x': x, 'src': src, 'dst': dst, 'edge_weight': edge_weight, 'L0_gnn_W1': _L0_gnn_in['W1'], 'L0_gnn_b1': _L0_gnn_in['b1'], 'L0_gnn_W2': _L0_gnn_in['W2'], 'L0_gnn_b2': _L0_gnn_in['b2'], 'L0_gnn_U1': _L0_gnn_in['U1'], 'L0_gnn_c1': _L0_gnn_in['c1'], 'L0_gnn_U2': _L0_gnn_in['U2'], 'L0_gnn_c2': _L0_gnn_in['c2']}

def reference(x, src, dst, edge_weight, L0_gnn_W1, L0_gnn_b1, L0_gnn_W2, L0_gnn_b2, L0_gnn_U1, L0_gnn_c1, L0_gnn_U2, L0_gnn_c2):
    import jax
    import jax.numpy as jnp

    def _L0_gnn_ref(h, w, src, dst, W1, b1, W2, b2, U1, c1, U2, c2):
        import jax, jax.numpy as jnp
        import numpy as np
        N = 3125
        E = 25000
        D = 128
        n = h.shape[0]
        msg_in = jnp.concatenate([h[src], h[dst], w[:, None]], axis=1)
        msg = jax.nn.relu(msg_in @ W1 + b1) @ W2 + b2
        agg = jax.ops.segment_max(msg, dst, num_segments=n)
        deg = jax.ops.segment_sum(jnp.ones((dst.shape[0],), jnp.int32), dst, num_segments=n)
        agg = jnp.where((deg > 0)[:, None], agg, jnp.zeros((), h.dtype))
        upd_in = jnp.concatenate([h, agg], axis=1)
        return jax.nn.relu(upd_in @ U1 + c1) @ U2 + c2
    x = _layernorm(x + _L0_gnn_ref(x, edge_weight, src, dst, L0_gnn_W1, L0_gnn_b1, L0_gnn_W2, L0_gnn_b2, L0_gnn_U1, L0_gnn_c1, L0_gnn_U2, L0_gnn_c2), axis=-1)
    return x

_drawn_inputs = setup_inputs


def setup_inputs(seed=0):
    import zlib

    import numpy as np

    out = dict(_drawn_inputs(seed))
    spreads = {'L0_gnn_b1': (0.0, 0.8),
     'L0_gnn_b2': (0.0, 0.573),
     'L0_gnn_c1': (0.0, 0.1),
     'L0_gnn_c2': (0.0, 0.1)}
    factors = {'edge_weight': 64.0}
    for name, (base, spread) in spreads.items():
        noise = np.random.default_rng([zlib.crc32(name.encode()), seed]).standard_normal(out[name].shape)
        drawn = base * np.exp(spread * noise) if base else spread * noise
        out[name] = jnp.asarray(drawn.astype(out[name].dtype))
    for name, factor in factors.items():
        out[name] = (out[name] * factor).astype(out[name].dtype)
    return out
```

```python
import concourse.bass as bass
from concourse import mybir
from contextlib import ExitStack


def gnn_layer(nc, x, src, dst, edge_weight, W1, b1, W2, b2, U1, c1, U2, c2, out):
    F32, BF16, F16 = mybir.dt.float32, mybir.dt.bfloat16, mybir.dt.float16
    I32, U32 = mybir.dt.int32, mybir.dt.uint32
    ALU, ACT, AX = mybir.AluOpType, mybir.ActivationFunctionType, mybir.AxisListType

    N, D = x.shape
    E = src.shape[0]
    P = 128
    Q = 4
    CH = P * Q
    NC = -(-E // CH)
    assert N == E and D == P and NC % 2 == 0 and NC <= P
    EP = NC * CH
    TAIL = E - (NC - 1) * CH
    TAILP = TAIL // Q
    assert TAIL % Q == 0 and EP > N
    PAD_NODE = EP - 1
    RESTART = -3.0e38
    EPS = 1e-5

    w_rows = nc.dram_tensor("w_rows", (NC, 9, CH), BF16, kind="Internal").ap()
    restart_rows = nc.dram_tensor("restart_rows", (NC, CH), BF16, kind="Internal").ap()
    msg_rows = nc.dram_tensor("msg_rows", (EP + P, D), F32, kind="Internal").ap()

    with ExitStack() as ctx:
        def sb(name, shape, dt):
            return ctx.enter_context(nc.sbuf_tensor(name, shape, dt))

        def ps(name):
            return ctx.enter_context(nc.psum_tensor(name, [P, CH], F32))

        def sem(name):
            return ctx.enter_context(nc.semaphore(name))

        ident = sb("ident", [P, P], F32)
        ones = sb("ones", [P, P], F32)
        before = sb("before", [P, P], F32)
        zeros = sb("zeros", [P, CH], F32)
        zeros_b = sb("zeros_b", [P, CH], BF16)
        ones_b = sb("ones_b", [3, P], BF16)
        count_i = sb("count_i", [P, NC * Q], I32)
        count = sb("count", [P, NC * Q], F16)
        part_i = sb("part_i", [P, 1], I32)
        zero_row = sb("zero_row", [P, 1], F32)
        neg_zero_row = sb("neg_zero_row", [P, 1], F32)
        eps = sb("eps", [P, 1], F32)
        w1a, w1b = sb("w1a", [P, D], F32), sb("w1b", [P, D], F32)
        w2 = sb("w2", [P, D], F32)
        u1a, u1b = sb("u1a", [P, D], F32), sb("u1b", [P, D], F32)
        u2 = sb("u2", [P, D], F32)
        b1_col, c1_col = sb("b1_col", [P, 1], F32), sb("c1_col", [P, 1], F32)
        b2_bc = sb("b2_bc", [P, Q, D], F32)
        w1c_f = sb("w1c_f", [3, 2, D], F32)
        w1c_part = sb("w1c_part", [3, 3, D], BF16)
        w1c9 = sb("w1c9", [9, D], BF16)
        c2_f = sb("c2_f", [3, 2, Q * D], F32)
        c2_part = sb("c2_part", [3, 3, Q * D], BF16)
        c2_3 = sb("c2_3", [3, Q * D], BF16)

        src_i, dst_i, prev_i = (sb(n, [NC, CH], I32) for n in ("src_i", "dst_i", "prev_i"))
        src_f, dst_f = sb("src_f", [NC, CH], F32), sb("dst_f", [NC, CH], F32)
        w_f = sb("w_f", [NC, 3, CH], F32)
        w_part = sb("w_part", [NC, 3, CH], BF16)
        restart_f = sb("restart_f", [NC, CH], F32)
        restart_b = sb("restart_b", [NC, CH], BF16)
        src_idx, dst_idx = sb("src_idx", [P, NC, Q], I32), sb("dst_idx", [P, NC, Q], I32)
        dst_pad = sb("dst_pad", [P, NC, Q], I32)
        bin_a_i, bin_q_i = sb("bin_a_i", [P, NC, Q], I32), sb("bin_q_i", [P, NC, Q], I32)
        bin_b_i = sb("bin_b_i", [P, NC, Q], I32)
        bin_a, bin_b = sb("bin_a", [P, NC, Q], F32), sb("bin_b", [P, NC, Q], F32)
        hist = sb("hist", [P, NC, Q], F32)
        hist_p = sb("hist_p", [P, NC], F32)
        total = sb("total", [P, NC], F32)
        total_scan = sb("total_scan", [P, NC], F32)
        base = sb("base", [P, NC], F32)
        ends = sb("ends", [P, NC, Q], F32)
        ends_off = sb("ends_off", [P, NC, Q], F32)
        ends_sel = sb("ends_sel", [P, NC, Q], F32)
        end_idx = sb("end_idx", [P, NC, Q], I32)

        stage = sb("stage", [P, 2, 2 * Q], I32)
        src_rows, dst_rows = sb("src_rows", [P, 2, Q, D], F32), sb("dst_rows", [P, 2, Q, D], F32)
        src_T, dst_T = sb("src_T", [P, 2, CH], F32), sb("dst_T", [P, 2, CH], F32)
        w9 = sb("w9", [9, 2, CH], BF16)
        restart = sb("restart", [P, 2, CH], BF16)
        hid_T = sb("hid_T", [P, 2, CH], F32)
        max_T = sb("max_T", [P, 2, CH], F32)
        max_rows = sb("max_rows", [P, 2, Q, D], F32)
        hot_a = sb("hot_a", [P, 2, Q, NC * Q], BF16)
        hot_b = sb("hot_b", [P, 2, Q, P], BF16)
        x_rows = sb("x_rows", [P, 2, Q, D], F32)
        sum_rows = sb("sum_rows", [P, 2, Q, D], F32)
        out_rows = sb("out_rows", [P, 2, Q, D], F32)
        stats = sb("stats", [P, 2, Q, 6], F32)
        mean_var = sb("mean_var", [P, 2, Q, 2], F32)
        std, rstd = sb("std", [P, 2, Q], F32), sb("rstd", [P, 2, Q], F32)

        src_ps, dst_ps, hid_ps, msg_ps = ps("src_ps"), ps("dst_ps"), ps("hid_ps"), ps("msg_ps")
        row_ps, hist_ps, tot_ps = ps("row_ps"), ps("hist_ps"), ps("tot_ps")

        s_const, s_fill, s_lists, s_weights, s_small = (sem(n) for n in ("s_const", "s_fill", "s_lists", "s_weights", "s_small"))
        s_dve = sem("s_dve")
        s_lists_T, s_split, s_scratch, s_moved = sem("s_lists_T"), sem("s_split"), sem("s_scratch"), sem("s_moved")
        s_lists_ready, s_lists_f = sem("s_lists_ready"), sem("s_lists_f")
        s_src_in, s_dst_in = [sem(f"s_src_in{k}") for k in range(2)], [sem(f"s_dst_in{k}") for k in range(2)]
        s_w_in, s_restart_in = [sem(f"s_w_in{k}") for k in range(2)], [sem(f"s_restart_in{k}") for k in range(2)]
        s_rows_out = [sem(f"s_rows_out{k}") for k in range(2)]
        s_staged, s_turned, s_src_T, s_dst_T = sem("s_staged"), sem("s_turned"), sem("s_src_T"), sem("s_dst_T")
        s_hid_mm, s_hid, s_msg_mm, s_max, s_max_turned, s_rows = (sem(n) for n in ("s_hid_mm", "s_hid", "s_msg_mm", "s_max", "s_max_turned", "s_rows"))
        s_hot, s_hot_used = sem("s_hot"), sem("s_hot_used")
        s_hist, s_prefix = sem("s_hist"), sem("s_prefix")
        s_agg_in, s_x_in = [sem(f"s_agg_in{k}") for k in range(2)], [sem(f"s_x_in{k}") for k in range(2)]
        s_out = [sem(f"s_out{k}") for k in range(2)]
        s_nstaged, s_nturned, s_x_T, s_agg_T = sem("s_nstaged"), sem("s_nturned"), sem("s_x_T"), sem("s_agg_T")
        s_upd_mm, s_upd, s_y_mm, s_sum, s_stat, s_std, s_rstd, s_out_ready = (
            sem(n) for n in ("s_upd_mm", "s_upd", "s_y_mm", "s_sum", "s_stat", "s_std", "s_rstd", "s_out_ready"))

        block = ctx.enter_context(nc.Block())

        def chunks(eng, step):
            step(0, 0)
            step(1, 1)
            with eng.Fori(2, NC - 1, 2) as c:
                step(c, 0)
                step(c + 1, 1)

        def node_chunks(eng, step):
            step(0, 0, P)
            step(1, 1, P)
            with eng.Fori(2, NC - 3, 2) as c:
                step(c, 0, P)
                step(c + 1, 1, P)
            step(NC - 2, 0, P)
            step(NC - 1, 1, TAILP)

        def later(c, lag):
            return not isinstance(c, int) or c >= lag

        def slot_dmas(c, slot, per=1):
            return ((c - slot) // 2 + 1) * 16 * per

        @block.gpsimd
        def _(pool):
            pool.memset(ident[:, :], 0.0)
            pool.memset(before[:, :], 0.0)
            pool.memset(ones[:, :], 1.0)
            pool.memset(ones_b[:, :], 1.0)
            pool.memset(zeros[:, :], 0.0)
            pool.memset(zeros_b[:, :], 0.0)
            pool.memset(eps[:, :], EPS)
            pool.memset(w_f[:, :, :], 0.0)
            pool.iota(src_i[:, :], pattern=[[0, CH]], base=0, channel_multiplier=0)
            pool.iota(dst_i[:, :], pattern=[[0, CH]], base=PAD_NODE, channel_multiplier=0)
            pool.iota(prev_i[:, :], pattern=[[0, CH]], base=PAD_NODE, channel_multiplier=0)
            pool.iota(count_i[:, :], pattern=[[1, NC * Q]], base=0, channel_multiplier=0)
            pool.iota(part_i[:, :], pattern=[[0, 1]], base=EP, channel_multiplier=1).then_inc(s_fill, 1)
            pool.wait_ge(s_fill, 1)
            pool.affine_select(out=ident[:, :], in_=ident[:, :], pattern=[[-1, P]], compare_op=ALU.not_equal,
                               fill=1.0, base=0, channel_multiplier=1)
            pool.affine_select(out=before[:, :], in_=before[:, :], pattern=[[-1, P]], compare_op=ALU.is_ge,
                               fill=1.0, base=0, channel_multiplier=1).then_inc(s_const, 1)

            def gather(c, slot):
                pool.wait_ge(s_staged, c + 1)
                if later(c, 2):
                    pool.nop(nofuse=True)
                    pool.wait_ge(s_turned, c - 1)
                pool.nop(nofuse=True)
                for q in range(Q):
                    pool.indirect_dma_start(
                        out=src_rows[:, slot, q, :], out_offset=None, in_=x[:, :],
                        in_offset=bass.IndirectOffsetOnAxis(ap=stage[:, slot, q:q + 1].bitcast(U32), axis=0),
                    ).then_inc(s_src_in[slot], 16)
                for q in range(Q):
                    pool.indirect_dma_start(
                        out=dst_rows[:, slot, q, :], out_offset=None, in_=x[:, :],
                        in_offset=bass.IndirectOffsetOnAxis(ap=stage[:, slot, Q + q:Q + q + 1].bitcast(U32), axis=0),
                    ).then_inc(s_dst_in[slot], 16)

            chunks(pool, gather)

            for slot in range(2):
                pool.wait_ge(s_rows_out[slot], 16 * (NC // 2))
            pool.wait_ge(s_scratch, 16 * 5)

            def gather_agg(c, slot, parts):
                pool.wait_ge(s_nstaged, c + 1)
                if later(c, 2):
                    pool.nop(nofuse=True)
                    pool.wait_ge(s_nturned, c - 1)
                pool.nop(nofuse=True)
                for q in range(Q):
                    pool.indirect_dma_start(
                        out=src_rows[0:parts, slot, q, :], out_offset=None, in_=msg_rows[:, :],
                        in_offset=bass.IndirectOffsetOnAxis(ap=stage[0:parts, slot, q:q + 1].bitcast(U32), axis=0),
                    ).then_inc(s_agg_in[slot], 16)

            node_chunks(pool, gather_agg)

        @block.sync
        def _(sp):
            sp.wait_ge(s_fill, 1)
            full = (NC - 1) * CH
            for lst, tile in ((src, src_i), (dst, dst_i)):
                sp.dma_start(tile[0:NC - 1, :], lst[0:full].rearrange("(c j) -> c j", j=CH)).then_inc(s_lists, 16)
                sp.dma_start(tile[NC - 1:NC, 0:TAIL], lst[full:E].rearrange("(c j) -> c j", c=1)).then_inc(s_lists, 16)
            sp.dma_start(w_f[0:NC - 1, 0, :], edge_weight[0:full].rearrange("(c j) -> c j", j=CH)).then_inc(s_lists, 16)
            sp.dma_start(w_f[NC - 1:NC, 0, 0:TAIL], edge_weight[full:E].rearrange("(c j) -> c j", c=1)).then_inc(s_lists, 16)
            sp.dma_start(prev_i[0:1, 0:1], dst[0:1].rearrange("(c j) -> c j", c=1)).then_inc(s_lists, 16)
            sp.dma_start(prev_i[0:1, 1:CH], dst[0:CH - 1].rearrange("(c j) -> c j", c=1)).then_inc(s_lists, 16)
            sp.dma_start(prev_i[1:NC - 1, :], dst[CH - 1:full - 1].rearrange("(c j) -> c j", j=CH)).then_inc(s_lists, 16)
            sp.dma_start(prev_i[NC - 1:NC, 0:TAIL], dst[full - 1:E - 1].rearrange("(c j) -> c j", c=1)).then_inc(s_lists, 16)
            sp.dma_start(msg_rows[EP:EP + P, :], zeros[:, 0:D]).then_inc(s_scratch, 16)
            sp.wait_ge(s_split, 2)
            for k in range(3):
                sp.dma_start(w_rows[:, 3 * k:3 * k + 3, :], w_part[:, :, :]).then_inc(s_scratch, 16)
            sp.dma_start(restart_rows, restart_b[:, :]).then_inc(s_scratch, 16)
            sp.wait_ge(s_scratch, 16 * 5)

            def load(c, slot):
                if later(c, 2):
                    sp.wait_ge(s_hid_mm, c - 1)
                sp.dma_start(w9[:, slot, :], w_rows[bass.ds(c, 1), :, :].rearrange("a r j -> (a r) j")).then_inc(s_w_in[slot], 16)
                if later(c, 2):
                    sp.wait_ge(s_max, c - 1)
                sp.dma_start(restart[:, slot, :], restart_rows[bass.ds(c, 1), :].to_broadcast([P, CH])).then_inc(s_restart_in[slot], 16)

            def store(c, slot):
                sp.wait_ge(s_rows, c + 1)
                sp.dma_start(msg_rows[bass.ds(c * CH, CH), :].rearrange("(p q) f -> p (q f)", q=Q),
                             max_rows[:, slot, :, :].rearrange("p q f -> p (q f)")).then_inc(s_rows_out[slot], 16)

            load(0, 0)
            load(1, 1)
            store(0, 0)
            with sp.Fori(2, NC - 1, 2) as c:
                load(c, 0)
                store(c - 1, 1)
                load(c + 1, 1)
                store(c, 0)
            store(NC - 1, 1)

            def load_x(c, slot, parts):
                if later(c, 2):
                    sp.wait_ge(s_sum, c - 1)
                sp.dma_start(x_rows[0:parts, slot, :, :].rearrange("p q f -> p (q f)"),
                             x[bass.ds(c * CH, parts * Q), :].rearrange("(p q) f -> p (q f)", q=Q)).then_inc(s_x_in[slot], 16)

            def store_out(c, slot, parts):
                sp.wait_ge(s_out_ready, c + 1)
                sp.dma_start(out[bass.ds(c * CH, parts * Q), :].rearrange("(p q) f -> p (q f)", q=Q),
                             out_rows[0:parts, slot, :, :].rearrange("p q f -> p (q f)")).then_inc(s_out[slot], 16)

            load_x(0, 0, P)
            load_x(1, 1, P)
            store_out(0, 0, P)
            with sp.Fori(2, NC - 3, 2) as c:
                load_x(c, 0, P)
                store_out(c - 1, 1, P)
                load_x(c + 1, 1, P)
                store_out(c, 0, P)
            load_x(NC - 2, 0, P)
            store_out(NC - 3, 1, P)
            load_x(NC - 1, 1, TAILP)
            store_out(NC - 2, 0, P)
            store_out(NC - 1, 1, TAILP)
            for slot in range(2):
                sp.wait_ge(s_out[slot], 16 * (NC // 2))

        @block.scalar
        def _(act):
            for tile, part in ((w1a, W1[0:D, :]), (w1b, W1[D:2 * D, :]), (w2, W2[:, :]),
                               (u1a, U1[0:D, :]), (u1b, U1[D:2 * D, :]), (u2, U2[:, :])):
                act.dma_start(tile[:, :], part).then_inc(s_weights, 16)
            act.dma_start(b1_col[:, :], b1.rearrange("(p a) -> p a", a=1)).then_inc(s_weights, 16)
            act.dma_start(c1_col[:, :], c1.rearrange("(p a) -> p a", a=1)).then_inc(s_weights, 16)
            for q in range(Q):
                act.dma_start(b2_bc[:, q, :], b2.rearrange("(a f) -> a f", a=1).to_broadcast([P, D])).then_inc(s_weights, 16)
                act.dma_start(c2_f[:, 0, q * D:(q + 1) * D], c2.rearrange("(a f) -> a f", a=1).to_broadcast([3, D])).then_inc(s_small, 16)
            act.dma_start(w1c_f[:, 0, :], W1[2 * D:2 * D + 1, :].to_broadcast([3, D])).then_inc(s_small, 16)
            act.wait_ge(s_split, 1)
            for k in range(3):
                act.dma_start(w1c9[3 * k:3 * k + 3, :], w1c_part[:, k, :]).then_inc(s_moved, 16)
                act.dma_start(c2_3[k:k + 1, :], c2_part[0:1, k, :]).then_inc(s_moved, 16)
            act.wait_ge(s_weights, 16 * 12)

            def edge_step(c, slot):
                act.wait_ge(s_turned, c + 1)
                if later(c, 2):
                    act.wait_ge(s_hid_mm, c - 1)
                act.activation(src_T[:, slot, :], src_ps[:, :], ACT.Copy).then_inc(s_src_T, 1)
                act.wait_ge(s_hid_mm, c + 1)
                if later(c, 2):
                    act.wait_ge(s_msg_mm, c - 1)
                act.activation(hid_T[:, slot, :], hid_ps[:, :], ACT.Relu, bias=b1_col[:, 0:1]).then_inc(s_hid, 1)

            chunks(act, edge_step)

            def node_step(c, slot, parts):
                act.wait_ge(s_nturned, c + 1)
                if later(c, 2):
                    act.wait_ge(s_upd_mm, c - 1)
                act.activation(src_T[:, slot, :].rearrange("f (q p) -> f q p", q=Q)[:, :, 0:parts],
                               src_ps[:, :].rearrange("f (q p) -> f q p", q=Q)[:, :, 0:parts], ACT.Copy).then_inc(s_x_T, 1)
                act.wait_ge(s_upd_mm, c + 1)
                if later(c, 2):
                    act.wait_ge(s_y_mm, c - 1)
                act.activation(hid_T[:, slot, :], hid_ps[:, :], ACT.Relu, bias=c1_col[:, 0:1]).then_inc(s_upd, 1)
                act.wait_ge(s_stat, c + 1)
                act.activation(std[0:parts, slot, :], mean_var[0:parts, slot, :, 1], ACT.Sqrt,
                               bias=eps[0:parts, 0:1]).then_inc(s_std, 1)

            node_chunks(act, node_step)

        @block.vector
        def _(dve):
            steps = [0]

            def own(ins):
                steps[0] += 1
                ins.then_inc(s_dve, 1)
                dve.wait_ge(s_dve, steps[0])

            def split(part, value, rest):
                own(dve.tensor_copy(part(0), value))
                own(dve.tensor_tensor(rest, value, part(0), ALU.subtract))
                own(dve.tensor_copy(part(1), rest))
                own(dve.tensor_tensor(value, rest, part(1), ALU.subtract))
                return dve.tensor_copy(part(2), value)

            dve.wait_ge(s_small, 16 * 5)
            split(lambda k: c2_part[:, k, :], c2_f[:, 0, :], c2_f[:, 1, :])
            split(lambda k: w1c_part[:, k, :], w1c_f[:, 0, :], w1c_f[:, 1, :]).then_inc(s_split, 1)
            dve.wait_ge(s_lists, 16 * 10)
            dve.tensor_copy(src_f[:, :], src_i[:, :])
            dve.tensor_copy(dst_f[:, :], dst_i[:, :]).then_inc(s_lists_f, 1)
            own(dve.tensor_tensor(restart_f[:, :], dst_i[:, :], prev_i[:, :], ALU.not_equal))
            own(dve.tensor_scalar(restart_b[:, :], restart_f[:, :], RESTART, None, ALU.mult))
            split(lambda k: w_part[:, k, :], w_f[:, 0, :], w_f[:, 1, :]).then_inc(s_split, 1)
            dve.wait_ge(s_const, 1)
            dve.tensor_copy(count[:, :], count_i[:, :])
            own(dve.tensor_copy(zero_row[:, :], part_i[:, :]))
            dve.tensor_scalar(neg_zero_row[:, :], zero_row[:, :], -1.0, -1.0, ALU.mult, ALU.add)
            by_q = "p (q c) -> p c q"
            dve.wait_ge(s_lists_T, 1)
            dve.tensor_copy(src_idx[:, :, :], src_ps[:, 0:NC * Q].rearrange(by_q, q=Q))
            dve.tensor_scalar(dst_idx[:, :, :], dst_ps[:, 0:NC * Q].rearrange(by_q, q=Q), float(N - 1), None, ALU.min)
            own(dve.tensor_copy(dst_pad[:, :, :], dst_ps[:, 0:NC * Q].rearrange(by_q, q=Q)))
            dve.tensor_scalar(bin_a_i[:, :, :], dst_pad[:, :, :], 9, 2, ALU.logical_shift_right, ALU.logical_shift_left)
            dve.tensor_scalar(bin_q_i[:, :, :], dst_pad[:, :, :], 3, None, ALU.bitwise_and)
            own(dve.tensor_scalar(bin_b_i[:, :, :], dst_pad[:, :, :], 2, P - 1, ALU.logical_shift_right, ALU.bitwise_and))
            dve.tensor_copy(bin_b[:, :, :], bin_b_i[:, :, :])
            own(dve.tensor_tensor(bin_a[:, :, :], bin_a_i[:, :, :], bin_q_i[:, :, :], ALU.add))
            dve.tensor_copy(stage[:, 0, 0:Q], src_idx[:, 0, :])
            dve.tensor_copy(stage[:, 0, Q:2 * Q], dst_idx[:, 0, :]).then_inc(s_staged, 1)
            dve.tensor_copy(stage[:, 1, 0:Q], src_idx[:, 1, :])
            dve.tensor_copy(stage[:, 1, Q:2 * Q], dst_idx[:, 1, :]).then_inc(s_staged, 1)
            dve.wait_ge(s_weights, 16 * 12)

            def edge_step(c, slot, stages=True):
                if later(c, 2):
                    dve.wait_ge(s_hot_used, c - 1)
                for q in range(Q):
                    dve.tensor_scalar(hot_a[:, slot, q, :], count[:, :], bin_a[:, bass.ds(c, 1), q], None, ALU.is_equal)
                    last = dve.tensor_scalar(hot_b[:, slot, q, :], count[:, 0:P], bin_b[:, bass.ds(c, 1), q], None, ALU.is_equal)
                last.then_inc(s_hot, 1)
                dve.wait_ge(s_turned, c + 1)
                if later(c, 2):
                    dve.wait_ge(s_hid_mm, c - 1)
                dve.tensor_copy(dst_T[:, slot, :], dst_ps[:, :]).then_inc(s_dst_T, 1)
                if stages:
                    dve.tensor_copy(stage[:, slot, 0:Q], src_idx[:, bass.ds(c + 2, 1), :].rearrange("p a q -> p (a q)"))
                    dve.tensor_copy(stage[:, slot, Q:2 * Q], dst_idx[:, bass.ds(c + 2, 1), :].rearrange("p a q -> p (a q)")).then_inc(s_staged, 1)
                dve.wait_ge(s_msg_mm, c + 1)
                dve.wait_ge(s_restart_in[slot], slot_dmas(c, slot))
                if later(c, 2):
                    dve.wait_ge(s_max_turned, c - 1)
                if later(c, 1):
                    dve.wait_ge(s_max, c)
                dve.tensor_tensor_scan(
                    max_T[:, slot, :], restart[:, slot, :], msg_ps[:, :],
                    max_T[:, 1 - slot, CH - 1:CH] if later(c, 1) else RESTART, ALU.add, ALU.max).then_inc(s_max, 1)
                dve.wait_ge(s_max_turned, c + 1)
                if later(c, 2):
                    dve.wait_ge(s_rows_out[slot], slot_dmas(c - 2, slot))
                dve.tensor_tensor(max_rows[:, slot, :, :], row_ps[:, :].rearrange("p (q f) -> p q f", q=Q),
                                  b2_bc[:, :, :], ALU.add).then_inc(s_rows, 1)

            edge_step(0, 0)
            edge_step(1, 1)
            with dve.Fori(2, NC - 3, 2) as c:
                edge_step(c, 0)
                edge_step(c + 1, 1)
            edge_step(NC - 2, 0, stages=False)
            edge_step(NC - 1, 1, stages=False)

            dve.wait_ge(s_hot_used, NC + 1)
            own(dve.tensor_copy(hist[:, :, :], hist_ps[:, 0:NC * Q].rearrange("p (c q) -> p c q", q=Q)))
            dve.tensor_reduce(hist_p[:, :], hist[:, :, :], AX.X, ALU.add).then_inc(s_hist, 1)
            dve.wait_ge(s_prefix, 1)
            own(dve.tensor_copy(total[:, :], tot_ps[:, 0:NC]))
            own(dve.tensor_tensor_scan(total_scan[:, :], total[:, :], zeros[:, 0:NC], 0.0, ALU.add, ALU.add))
            own(dve.tensor_tensor(base[:, :], total_scan[:, :], total[:, :], ALU.subtract))
            own(dve.tensor_tensor(base[:, :], base[:, :], row_ps[:, 0:NC], ALU.add))
            own(dve.tensor_tensor(ends[:, :, 0], base[:, :], hist[:, :, 0], ALU.add))
            for q in range(1, Q):
                own(dve.tensor_tensor(ends[:, :, q], ends[:, :, q - 1], hist[:, :, q], ALU.add))
            own(dve.tensor_scalar(ends_off[:, :, :], ends[:, :, :], neg_zero_row[:, 0:1], None, ALU.add))
            own(dve.scalar_tensor_tensor(out=ends_sel[:, :, :], in0=hist[:, :, :], scalar=1.0, in1=ends_off[:, :, :],
                                         op0=ALU.min, op1=ALU.mult))
            own(dve.tensor_scalar(end_idx[:, :, :], ends_sel[:, :, :], zero_row[:, 0:1], None, ALU.add))
            dve.tensor_copy(stage[:, 0, 0:Q], end_idx[:, 0, :]).then_inc(s_nstaged, 1)
            dve.tensor_copy(stage[:, 1, 0:Q], end_idx[:, 1, :]).then_inc(s_nstaged, 1)

            def node_step(c, slot, parts, stages=True):
                qp = "f (q p) -> f q p"
                dve.wait_ge(s_nturned, c + 1)
                if later(c, 2):
                    dve.wait_ge(s_upd_mm, c - 1)
                dve.tensor_copy(dst_T[:, slot, :].rearrange(qp, q=Q)[:, :, 0:parts],
                                dst_ps[:, :].rearrange(qp, q=Q)[:, :, 0:parts]).then_inc(s_agg_T, 1)
                if stages:
                    dve.tensor_copy(stage[:, slot, 0:Q], end_idx[:, bass.ds(c + 2, 1), :].rearrange("p a q -> p (a q)")).then_inc(s_nstaged, 1)
                dve.wait_ge(s_y_mm, c + 1)
                if later(c, 2):
                    dve.wait_ge(s_rstd, 2 * (c - 1))
                dve.tensor_tensor(sum_rows[0:parts, slot, :, :], x_rows[0:parts, slot, :, :],
                                  msg_ps[0:parts, :].rearrange("p (q f) -> p q f", q=Q), ALU.add).then_inc(s_sum, 1)
                dve.wait_ge(s_sum, c + 1)
                for q in range(Q):
                    last = dve.bn_stats(stats[0:parts, slot, q, :], sum_rows[0:parts, slot, q, :])
                last.then_inc(s_rstd, 1)
                dve.wait_ge(s_rstd, 2 * c + 1)
                dve.nop(nofuse=True)
                for q in range(Q):
                    last = dve.bn_aggr(mean_var[0:parts, slot, q, :], stats[0:parts, slot, q, :])
                last.then_inc(s_stat, 1)
                dve.wait_ge(s_std, c + 1)
                dve.reciprocal(rstd[0:parts, slot, :], std[0:parts, slot, :]).then_inc(s_rstd, 1)
                dve.wait_ge(s_rstd, 2 * c + 2)
                if later(c, 2):
                    dve.wait_ge(s_out[slot], slot_dmas(c - 2, slot))
                for q in range(Q):
                    last = dve.tensor_scalar(out_rows[0:parts, slot, q, :], sum_rows[0:parts, slot, q, :],
                                             mean_var[0:parts, slot, q, 0:1], rstd[0:parts, slot, q:q + 1],
                                             ALU.subtract, ALU.mult)
                last.then_inc(s_out_ready, 1)

            node_step(0, 0, P)
            node_step(1, 1, P)
            with dve.Fori(2, NC - 3, 2) as c:
                node_step(c, 0, P)
                node_step(c + 1, 1, P)
            node_step(NC - 2, 0, P, stages=False)
            node_step(NC - 1, 1, TAILP, stages=False)

        @block.tensor
        def _(pe):
            pe.wait_ge(s_const, 1)
            pe.wait_ge(s_lists_f, 1)
            for tile, turned in ((src_f, src_ps), (dst_f, dst_ps)):
                by_q = tile[:, :].rearrange("c (p q) -> c q p", q=Q)
                for q in range(Q):
                    last = pe.transpose(turned[:, q * NC:(q + 1) * NC], by_q[:, q, :], ident[0:NC, 0:NC])
            last.then_inc(s_lists_T, 1)
            pe.wait_ge(s_weights, 16 * 12)
            pe.wait_ge(s_moved, 16 * 6)
            pe.matmul(hist_ps[:, 0:NC * Q], zeros_b[:, 0:P], zeros_b[:, 0:NC * Q], start=True, stop=False)

            def edge_step(c, slot):
                pe.wait_ge(s_src_in[slot], slot_dmas(c, slot, Q))
                if c == 0 if isinstance(c, int) else False:
                    pe.wait_ge(s_staged, 1)
                if later(c, 1):
                    pe.wait_ge(s_src_T, c)
                for q in range(Q):
                    pe.transpose(src_ps[:, q * P:(q + 1) * P], src_rows[:, slot, q, :], ident[:, :])
                pe.wait_ge(s_dst_in[slot], slot_dmas(c, slot, Q))
                if later(c, 1):
                    pe.wait_ge(s_dst_T, c)
                for q in range(Q):
                    last = pe.transpose(dst_ps[:, q * P:(q + 1) * P], dst_rows[:, slot, q, :], ident[:, :])
                last.then_inc(s_turned, 1)
                pe.wait_ge(s_hot, c + 1)
                for q in range(Q):
                    last = pe.matmul(hist_ps[:, 0:NC * Q], hot_b[:, slot, q, :], hot_a[:, slot, q, :], start=False, stop=False)
                last.then_inc(s_hot_used, 1)
                if later(c, 1):
                    pe.wait_ge(s_hid, c)
                pe.wait_ge(s_w_in[slot], slot_dmas(c, slot))
                pe.matmul(hid_ps[:, :], w1c9[:, :], w9[:, slot, :].rearrange("r (p q) -> r q p", q=Q), start=True, stop=False)
                pe.wait_ge(s_src_T, c + 1)
                pe.matmul(hid_ps[:, :], w1a[:, :], src_T[:, slot, :], start=False, stop=False)
                pe.wait_ge(s_dst_T, c + 1)
                pe.matmul(hid_ps[:, :], w1b[:, :], dst_T[:, slot, :], start=False, stop=True).then_inc(s_hid_mm, 1)
                pe.wait_ge(s_hid, c + 1)
                if later(c, 1):
                    pe.wait_ge(s_max, c)
                pe.matmul(msg_ps[:, :], w2[:, :], hid_T[:, slot, :].rearrange("f (q p) -> f p q", q=Q),
                          start=True, stop=True).then_inc(s_msg_mm, 1)
                pe.wait_ge(s_max, c + 1)
                if later(c, 1):
                    pe.wait_ge(s_rows, c)
                by_q = max_T[:, slot, :].rearrange("f (p q) -> f q p", q=Q)
                for q in range(Q):
                    last = pe.transpose(row_ps[:, q * D:(q + 1) * D], by_q[:, q, :], ident[:, :])
                last.then_inc(s_max_turned, 1)

            chunks(pe, edge_step)

            pe.matmul(hist_ps[:, 0:NC * Q], zeros_b[:, 0:P], zeros_b[:, 0:NC * Q], start=False, stop=True).then_inc(s_hot_used, 1)
            pe.wait_ge(s_hist, 1)
            pe.wait_ge(s_rows, NC)
            pe.matmul(row_ps[:, 0:NC], before[:, :], hist_p[:, :], start=True, stop=True)
            pe.matmul(tot_ps[:, 0:NC], ones[:, :], hist_p[:, :], start=True, stop=True).then_inc(s_prefix, 1)

            def node_step(c, slot, parts):
                pe.wait_ge(s_x_in[slot], slot_dmas(c, slot))
                pe.wait_ge(s_x_T, c) if later(c, 1) else pe.wait_ge(s_src_T, NC)
                for q in range(Q):
                    pe.transpose(src_ps[:, q * P:q * P + parts], x_rows[0:parts, slot, q, :], ident[0:parts, 0:parts])
                pe.wait_ge(s_agg_in[slot], slot_dmas(c, slot, Q))
                pe.wait_ge(s_agg_T, c) if later(c, 1) else pe.wait_ge(s_dst_T, NC)
                for q in range(Q):
                    last = pe.transpose(dst_ps[:, q * P:q * P + parts], src_rows[0:parts, slot, q, :], ident[0:parts, 0:parts])
                last.then_inc(s_nturned, 1)
                pe.wait_ge(s_upd, c) if later(c, 1) else pe.wait_ge(s_hid, NC)
                pe.wait_ge(s_x_T, c + 1)
                pe.matmul(hid_ps[:, :], u1a[:, :], src_T[:, slot, :], start=True, stop=False)
                pe.wait_ge(s_agg_T, c + 1)
                pe.matmul(hid_ps[:, :], u1b[:, :], dst_T[:, slot, :], start=False, stop=True).then_inc(s_upd_mm, 1)
                pe.wait_ge(s_sum, c) if later(c, 1) else pe.wait_ge(s_max, NC)
                pe.wait_ge(s_upd, c + 1)
                for q in range(Q):
                    pe.matmul(msg_ps[:, q * D:(q + 1) * D], ones_b[:, :], c2_3[:, 0:D], start=True, stop=False)
                    last = pe.matmul(msg_ps[:, q * D:(q + 1) * D], hid_T[:, slot, q * P:(q + 1) * P], u2[:, :],
                                     start=False, stop=True)
                last.then_inc(s_y_mm, 1)

            node_chunks(pe, node_step)


_INS = ['x', 'src', 'dst', 'edge_weight', 'L0_gnn_W1', 'L0_gnn_b1', 'L0_gnn_W2', 'L0_gnn_b2',
        'L0_gnn_U1', 'L0_gnn_c1', 'L0_gnn_U2', 'L0_gnn_c2']


def kernel(**inputs):
    import numpy as _np
    import concourse.bacc as _bacc
    from concourse import mybir as _mybir
    from concourse.bass_utils import run_bass_kernel_spmd as _run

    nc = _bacc.Bacc("TRN2", target_bir_lowering=False, num_devices=1)
    arrays, args = {}, []
    for name in _INS:
        a = _np.ascontiguousarray(inputs[name])
        arrays[f"in_{name}_dram"] = a
        args.append(nc.dram_tensor(f"in_{name}_dram", a.shape, _mybir.dt.from_np(a.dtype), kind="ExternalInput").ap())
    x = inputs['x']
    out = nc.dram_tensor("out_0_dram", tuple(x.shape), _mybir.dt.float32, kind="ExternalOutput").ap()
    gnn_layer(nc, *args, out)
    r = _run(nc, [arrays], core_ids=[0])
    return r.results[0]["out_0_dram"]
```

```python
import concourse.bass as bass
from concourse import mybir
from contextlib import ExitStack


def gnn_layer(nc, x, src, dst, edge_weight, W1, b1, W2, b2, U1, c1, U2, c2, out):
    F32, BF16, F16 = mybir.dt.float32, mybir.dt.bfloat16, mybir.dt.float16
    I32, U32 = mybir.dt.int32, mybir.dt.uint32
    ALU, ACT, AX = mybir.AluOpType, mybir.ActivationFunctionType, mybir.AxisListType

    N, D = x.shape
    E = src.shape[0]
    P = 128
    Q = 4
    CH = P * Q
    NC = -(-E // CH)
    assert N == E and D == P and NC % 2 == 0 and NC <= P
    EP = NC * CH
    TAIL = E - (NC - 1) * CH
    TAILP = TAIL // Q
    assert TAIL % Q == 0 and EP > N
    PAD_NODE = EP - 1
    RESTART = -3.0e38
    EPS = 1e-5
    SLOTS = 4

    w_rows = nc.dram_tensor("w_rows", (NC, 9, CH), BF16, kind="Internal").ap()
    restart_rows = nc.dram_tensor("restart_rows", (NC, CH), BF16, kind="Internal").ap()
    msg_rows = nc.dram_tensor("msg_rows", (EP + P, D), F32, kind="Internal").ap()

    with ExitStack() as ctx:
        def sb(name, shape, dt):
            return ctx.enter_context(nc.sbuf_tensor(name, shape, dt))

        def ps(name):
            return ctx.enter_context(nc.psum_tensor(name, [P, CH], F32))

        def sem(name):
            return ctx.enter_context(nc.semaphore(name))

        ident = sb("ident", [P, P], F32)
        ones = sb("ones", [P, P], F32)
        before = sb("before", [P, P], F32)
        zeros = sb("zeros", [P, CH], F32)
        zeros_b = sb("zeros_b", [P, CH], BF16)
        ones_b = sb("ones_b", [3, P], BF16)
        count_i = sb("count_i", [P, NC * Q], I32)
        count = sb("count", [P, NC * Q], F16)
        part_i = sb("part_i", [P, 1], I32)
        zero_row = sb("zero_row", [P, 1], F32)
        neg_zero_row = sb("neg_zero_row", [P, 1], F32)
        eps = sb("eps", [P, 1], F32)
        w1a, w1b = sb("w1a", [P, D], F32), sb("w1b", [P, D], F32)
        w2 = sb("w2", [P, D], F32)
        u1a, u1b = sb("u1a", [P, D], F32), sb("u1b", [P, D], F32)
        u2 = sb("u2", [P, D], F32)
        b1_col, c1_col = sb("b1_col", [P, 1], F32), sb("c1_col", [P, 1], F32)
        b2_bc = sb("b2_bc", [P, Q, D], F32)
        w1c_f = sb("w1c_f", [3, 2, D], F32)
        w1c_part = sb("w1c_part", [3, 3, D], BF16)
        w1c9 = sb("w1c9", [9, D], BF16)
        c2_f = sb("c2_f", [3, 2, Q * D], F32)
        c2_part = sb("c2_part", [3, 3, Q * D], BF16)
        c2_3 = sb("c2_3", [3, Q * D], BF16)

        src_i, dst_i, prev_i = (sb(n, [NC, CH], I32) for n in ("src_i", "dst_i", "prev_i"))
        src_f, dst_f = sb("src_f", [NC, CH], F32), sb("dst_f", [NC, CH], F32)
        w_f = sb("w_f", [NC, 3, CH], F32)
        w_part = sb("w_part", [NC, 3, CH], BF16)
        restart_f = sb("restart_f", [NC, CH], F32)
        restart_b = sb("restart_b", [NC, CH], BF16)
        src_idx, dst_idx = sb("src_idx", [P, NC, Q], I32), sb("dst_idx", [P, NC, Q], I32)
        dst_pad = sb("dst_pad", [P, NC, Q], I32)
        bin_a_i, bin_q_i = sb("bin_a_i", [P, NC, Q], I32), sb("bin_q_i", [P, NC, Q], I32)
        bin_b_i = sb("bin_b_i", [P, NC, Q], I32)
        bin_a, bin_b = sb("bin_a", [P, NC, Q], F32), sb("bin_b", [P, NC, Q], F32)
        hist = sb("hist", [P, NC, Q], F32)
        hist_p = sb("hist_p", [P, NC], F32)
        total = sb("total", [P, NC], F32)
        total_scan = sb("total_scan", [P, NC], F32)
        base = sb("base", [P, NC], F32)
        ends = sb("ends", [P, NC, Q], F32)
        ends_off = sb("ends_off", [P, NC, Q], F32)
        ends_sel = sb("ends_sel", [P, NC, Q], F32)
        end_idx = sb("end_idx", [P, NC, Q], I32)

        stage = sb("stage", [P, SLOTS, 2 * Q], I32)
        src_rows, dst_rows = sb("src_rows", [P, SLOTS, Q, D], F32), sb("dst_rows", [P, SLOTS, Q, D], F32)
        src_T, dst_T = sb("src_T", [P, 2, CH], F32), sb("dst_T", [P, 2, CH], F32)
        w9 = sb("w9", [9, 2, CH], BF16)
        restart = sb("restart", [P, 2, CH], BF16)
        hid_T = sb("hid_T", [P, 2, CH], F32)
        max_T = sb("max_T", [P, 2, CH], F32)
        max_rows = sb("max_rows", [P, 2, Q, D], F32)
        hot_a = sb("hot_a", [P, 2, Q, NC * Q], BF16)
        hot_b = sb("hot_b", [P, 2, Q, P], BF16)
        x_rows = sb("x_rows", [P, SLOTS, Q, D], F32)
        sum_rows = sb("sum_rows", [P, 2, Q, D], F32)
        out_rows = sb("out_rows", [P, 2, Q, D], F32)
        stats = sb("stats", [P, 2, Q, 6], F32)
        mean_var = sb("mean_var", [P, 2, Q, 2], F32)
        std, rstd = sb("std", [P, 2, Q], F32), sb("rstd", [P, 2, Q], F32)

        src_ps, dst_ps, hid_ps, msg_ps = ps("src_ps"), ps("dst_ps"), ps("hid_ps"), ps("msg_ps")
        row_ps, hist_ps, tot_ps = ps("row_ps"), ps("hist_ps"), ps("tot_ps")

        s_const, s_fill, s_lists, s_weights, s_small = (sem(n) for n in ("s_const", "s_fill", "s_lists", "s_weights", "s_small"))
        s_dve = sem("s_dve")
        s_lists_T, s_split, s_scratch, s_moved = sem("s_lists_T"), sem("s_split"), sem("s_scratch"), sem("s_moved")
        s_lists_ready, s_lists_f = sem("s_lists_ready"), sem("s_lists_f")
        s_src_in, s_dst_in = [sem(f"s_src_in{k}") for k in range(SLOTS)], [sem(f"s_dst_in{k}") for k in range(SLOTS)]
        s_w_in, s_restart_in = [sem(f"s_w_in{k}") for k in range(2)], [sem(f"s_restart_in{k}") for k in range(2)]
        s_rows_out = [sem(f"s_rows_out{k}") for k in range(2)]
        s_staged, s_turned, s_src_T, s_dst_T = sem("s_staged"), sem("s_turned"), sem("s_src_T"), sem("s_dst_T")
        s_hid_mm, s_hid, s_msg_mm, s_max, s_max_turned, s_rows = (sem(n) for n in ("s_hid_mm", "s_hid", "s_msg_mm", "s_max", "s_max_turned", "s_rows"))
        s_hot, s_hot_used = sem("s_hot"), sem("s_hot_used")
        s_hist, s_prefix = sem("s_hist"), sem("s_prefix")
        s_agg_in, s_x_in = [sem(f"s_agg_in{k}") for k in range(SLOTS)], [sem(f"s_x_in{k}") for k in range(SLOTS)]
        s_out = [sem(f"s_out{k}") for k in range(2)]
        s_nstaged, s_nturned, s_x_T, s_agg_T = sem("s_nstaged"), sem("s_nturned"), sem("s_x_T"), sem("s_agg_T")
        s_upd_mm, s_upd, s_y_mm, s_sum, s_moments, s_stat, s_std, s_rstd, s_out_ready = (
            sem(n) for n in ("s_upd_mm", "s_upd", "s_y_mm", "s_sum", "s_moments", "s_stat", "s_std", "s_rstd", "s_out_ready"))

        block = ctx.enter_context(nc.Block())

        def pipeline(eng, stages, tail=P):
            depth = max(lag for lag, _ in stages)
            head = SLOTS * (-(-(depth + SLOTS) // SLOTS))
            rest = head + (NC - SLOTS - head) // SLOTS * SLOTS

            def turn(t, turn_slot):
                for lag, step in stages:
                    c = t - lag
                    if isinstance(t, int) and not 0 <= c < NC:
                        continue
                    step(c, (turn_slot - lag) % SLOTS, tail if isinstance(c, int) and c == NC - 1 else P)

            for t in range(head):
                turn(t, t % SLOTS)
            with eng.Fori(head, rest - SLOTS + 1, SLOTS) as t:
                for k in range(SLOTS):
                    turn(t + k, k)
            for t in range(rest, NC + depth):
                turn(t, t % SLOTS)

        def later(c, lag):
            return not isinstance(c, int) or c >= lag

        def landed(c, slot, slots, per=1):
            return ((c - slot % slots) // slots + 1) * 16 * per

        @block.gpsimd
        def _(pool):
            pool.memset(ident[:, :], 0.0)
            pool.memset(before[:, :], 0.0)
            pool.memset(ones[:, :], 1.0)
            pool.memset(ones_b[:, :], 1.0)
            pool.memset(zeros[:, :], 0.0)
            pool.memset(zeros_b[:, :], 0.0)
            pool.memset(eps[:, :], EPS)
            pool.memset(w_f[:, :, :], 0.0)
            pool.iota(src_i[:, :], pattern=[[0, CH]], base=0, channel_multiplier=0)
            pool.iota(dst_i[:, :], pattern=[[0, CH]], base=PAD_NODE, channel_multiplier=0)
            pool.iota(prev_i[:, :], pattern=[[0, CH]], base=PAD_NODE, channel_multiplier=0)
            pool.iota(count_i[:, :], pattern=[[1, NC * Q]], base=0, channel_multiplier=0)
            pool.iota(part_i[:, :], pattern=[[0, 1]], base=EP, channel_multiplier=1).then_inc(s_fill, 1)
            pool.wait_ge(s_fill, 1)
            pool.affine_select(out=ident[:, :], in_=ident[:, :], pattern=[[-1, P]], compare_op=ALU.not_equal,
                               fill=1.0, base=0, channel_multiplier=1)
            pool.affine_select(out=before[:, :], in_=before[:, :], pattern=[[-1, P]], compare_op=ALU.is_ge,
                               fill=1.0, base=0, channel_multiplier=1).then_inc(s_const, 1)

            def gather(c, slot, parts):
                pool.wait_ge(s_staged, c + 1)
                pool.nop(nofuse=True)
                for q in range(Q):
                    pool.indirect_dma_start(
                        out=src_rows[:, slot, q, :], out_offset=None, in_=x[:, :],
                        in_offset=bass.IndirectOffsetOnAxis(ap=stage[:, slot, q:q + 1].bitcast(U32), axis=0),
                    ).then_inc(s_src_in[slot], 16)
                for q in range(Q):
                    pool.indirect_dma_start(
                        out=dst_rows[:, slot, q, :], out_offset=None, in_=x[:, :],
                        in_offset=bass.IndirectOffsetOnAxis(ap=stage[:, slot, Q + q:Q + q + 1].bitcast(U32), axis=0),
                    ).then_inc(s_dst_in[slot], 16)

            pipeline(pool, [(0, gather)])

            for slot in range(2):
                pool.wait_ge(s_rows_out[slot], 16 * (NC // 2))
            pool.wait_ge(s_scratch, 16 * 5)

            def gather_agg(c, slot, parts):
                pool.wait_ge(s_nstaged, c + 1)
                pool.nop(nofuse=True)
                for q in range(Q):
                    pool.indirect_dma_start(
                        out=src_rows[0:parts, slot, q, :], out_offset=None, in_=msg_rows[:, :],
                        in_offset=bass.IndirectOffsetOnAxis(ap=stage[0:parts, slot, q:q + 1].bitcast(U32), axis=0),
                    ).then_inc(s_agg_in[slot], 16)

            pipeline(pool, [(0, gather_agg)], tail=TAILP)

        @block.sync
        def _(sp):
            sp.wait_ge(s_fill, 1)
            full = (NC - 1) * CH
            for lst, tile in ((src, src_i), (dst, dst_i)):
                sp.dma_start(tile[0:NC - 1, :], lst[0:full].rearrange("(c j) -> c j", j=CH)).then_inc(s_lists, 16)
                sp.dma_start(tile[NC - 1:NC, 0:TAIL], lst[full:E].rearrange("(c j) -> c j", c=1)).then_inc(s_lists, 16)
            sp.dma_start(w_f[0:NC - 1, 0, :], edge_weight[0:full].rearrange("(c j) -> c j", j=CH)).then_inc(s_lists, 16)
            sp.dma_start(w_f[NC - 1:NC, 0, 0:TAIL], edge_weight[full:E].rearrange("(c j) -> c j", c=1)).then_inc(s_lists, 16)
            sp.dma_start(prev_i[0:1, 0:1], dst[0:1].rearrange("(c j) -> c j", c=1)).then_inc(s_lists, 16)
            sp.dma_start(prev_i[0:1, 1:CH], dst[0:CH - 1].rearrange("(c j) -> c j", c=1)).then_inc(s_lists, 16)
            sp.dma_start(prev_i[1:NC - 1, :], dst[CH - 1:full - 1].rearrange("(c j) -> c j", j=CH)).then_inc(s_lists, 16)
            sp.dma_start(prev_i[NC - 1:NC, 0:TAIL], dst[full - 1:E - 1].rearrange("(c j) -> c j", c=1)).then_inc(s_lists, 16)
            sp.dma_start(msg_rows[EP:EP + P, :], zeros[:, 0:D]).then_inc(s_scratch, 16)
            sp.wait_ge(s_split, 2)
            for k in range(3):
                sp.dma_start(w_rows[:, 3 * k:3 * k + 3, :], w_part[:, :, :]).then_inc(s_scratch, 16)
            sp.dma_start(restart_rows, restart_b[:, :]).then_inc(s_scratch, 16)
            sp.wait_ge(s_scratch, 16 * 5)

            def load(c, slot, parts):
                two = slot % 2
                if later(c, 2):
                    sp.wait_ge(s_hid_mm, c - 1)
                sp.dma_start(w9[:, two, :], w_rows[bass.ds(c, 1), :, :].rearrange("a r j -> (a r) j")).then_inc(s_w_in[two], 16)
                if later(c, 2):
                    sp.wait_ge(s_max, c - 1)
                sp.dma_start(restart[:, two, :], restart_rows[bass.ds(c, 1), :].to_broadcast([P, CH])).then_inc(s_restart_in[two], 16)

            def store(c, slot, parts):
                sp.wait_ge(s_rows, c + 1)
                sp.dma_start(msg_rows[bass.ds(c * CH, CH), :].rearrange("(p q) f -> p (q f)", q=Q),
                             max_rows[:, slot % 2, :, :].rearrange("p q f -> p (q f)")).then_inc(s_rows_out[slot % 2], 16)

            pipeline(sp, [(0, load), (2, store)])

            def load_x(c, slot, parts):
                if later(c, SLOTS):
                    sp.wait_ge(s_sum, c - SLOTS + 1)
                sp.dma_start(x_rows[0:parts, slot, :, :].rearrange("p q f -> p (q f)"),
                             x[bass.ds(c * CH, parts * Q), :].rearrange("(p q) f -> p (q f)", q=Q)).then_inc(s_x_in[slot], 16)

            def store_out(c, slot, parts):
                sp.wait_ge(s_out_ready, c + 1)
                sp.dma_start(out[bass.ds(c * CH, parts * Q), :].rearrange("(p q) f -> p (q f)", q=Q),
                             out_rows[0:parts, slot % 2, :, :].rearrange("p q f -> p (q f)")).then_inc(s_out[slot % 2], 16)

            pipeline(sp, [(0, load_x), (5, store_out)], tail=TAILP)
            for two in range(2):
                sp.wait_ge(s_out[two], 16 * (NC // 2))

        @block.scalar
        def _(act):
            for tile, part in ((w1a, W1[0:D, :]), (w1b, W1[D:2 * D, :]), (w2, W2[:, :]),
                               (u1a, U1[0:D, :]), (u1b, U1[D:2 * D, :]), (u2, U2[:, :])):
                act.dma_start(tile[:, :], part).then_inc(s_weights, 16)
            act.dma_start(b1_col[:, :], b1.rearrange("(p a) -> p a", a=1)).then_inc(s_weights, 16)
            act.dma_start(c1_col[:, :], c1.rearrange("(p a) -> p a", a=1)).then_inc(s_weights, 16)
            for q in range(Q):
                act.dma_start(b2_bc[:, q, :], b2.rearrange("(a f) -> a f", a=1).to_broadcast([P, D])).then_inc(s_weights, 16)
                act.dma_start(c2_f[:, 0, q * D:(q + 1) * D], c2.rearrange("(a f) -> a f", a=1).to_broadcast([3, D])).then_inc(s_small, 16)
            act.dma_start(w1c_f[:, 0, :], W1[2 * D:2 * D + 1, :].to_broadcast([3, D])).then_inc(s_small, 16)
            act.wait_ge(s_split, 1)
            for k in range(3):
                act.dma_start(w1c9[3 * k:3 * k + 3, :], w1c_part[:, k, :]).then_inc(s_moved, 16)
                act.dma_start(c2_3[k:k + 1, :], c2_part[0:1, k, :]).then_inc(s_moved, 16)
            act.wait_ge(s_weights, 16 * 12)

            def src_columns(c, slot, parts):
                act.wait_ge(s_turned, c + 1)
                if later(c, 2):
                    act.wait_ge(s_hid_mm, c - 1)
                act.activation(src_T[:, slot % 2, :], src_ps[:, :], ACT.Copy).then_inc(s_src_T, 1)

            def hidden(c, slot, parts):
                act.wait_ge(s_hid_mm, c + 1)
                if later(c, 2):
                    act.wait_ge(s_msg_mm, c - 1)
                act.activation(hid_T[:, slot % 2, :], hid_ps[:, :], ACT.Relu, bias=b1_col[:, 0:1]).then_inc(s_hid, 1)

            pipeline(act, [(0, src_columns), (1, hidden)])

            def x_columns(c, slot, parts):
                act.wait_ge(s_nturned, c + 1)
                if later(c, 2):
                    act.wait_ge(s_upd_mm, c - 1)
                act.activation(src_T[:, slot % 2, :].rearrange("f (q p) -> f q p", q=Q)[:, :, 0:parts],
                               src_ps[:, :].rearrange("f (q p) -> f q p", q=Q)[:, :, 0:parts], ACT.Copy).then_inc(s_x_T, 1)

            def update_hidden(c, slot, parts):
                act.wait_ge(s_upd_mm, c + 1)
                if later(c, 2):
                    act.wait_ge(s_y_mm, c - 1)
                act.activation(hid_T[:, slot % 2, :], hid_ps[:, :], ACT.Relu, bias=c1_col[:, 0:1]).then_inc(s_upd, 1)

            def deviation(c, slot, parts):
                act.wait_ge(s_stat, c + 1)
                act.activation(std[0:parts, slot % 2, :], mean_var[0:parts, slot % 2, :, 1], ACT.Sqrt,
                               bias=eps[0:parts, 0:1]).then_inc(s_std, 1)

            pipeline(act, [(3, deviation), (0, x_columns), (1, update_hidden)], tail=TAILP)

        @block.vector
        def _(dve):
            steps = [0]

            def own(ins):
                steps[0] += 1
                ins.then_inc(s_dve, 1)
                dve.wait_ge(s_dve, steps[0])

            def split(part, value, rest):
                own(dve.tensor_copy(part(0), value))
                own(dve.tensor_tensor(rest, value, part(0), ALU.subtract))
                own(dve.tensor_copy(part(1), rest))
                own(dve.tensor_tensor(value, rest, part(1), ALU.subtract))
                return dve.tensor_copy(part(2), value)

            dve.wait_ge(s_small, 16 * 5)
            split(lambda k: c2_part[:, k, :], c2_f[:, 0, :], c2_f[:, 1, :])
            split(lambda k: w1c_part[:, k, :], w1c_f[:, 0, :], w1c_f[:, 1, :]).then_inc(s_split, 1)
            dve.wait_ge(s_lists, 16 * 10)
            dve.tensor_copy(src_f[:, :], src_i[:, :])
            dve.tensor_copy(dst_f[:, :], dst_i[:, :]).then_inc(s_lists_f, 1)
            own(dve.tensor_tensor(restart_f[:, :], dst_i[:, :], prev_i[:, :], ALU.not_equal))
            own(dve.tensor_scalar(restart_b[:, :], restart_f[:, :], RESTART, None, ALU.mult))
            split(lambda k: w_part[:, k, :], w_f[:, 0, :], w_f[:, 1, :]).then_inc(s_split, 1)
            dve.wait_ge(s_const, 1)
            dve.tensor_copy(count[:, :], count_i[:, :])
            own(dve.tensor_copy(zero_row[:, :], part_i[:, :]))
            dve.tensor_scalar(neg_zero_row[:, :], zero_row[:, :], -1.0, -1.0, ALU.mult, ALU.add)
            by_q = "p (q c) -> p c q"
            dve.wait_ge(s_lists_T, 1)
            dve.tensor_copy(src_idx[:, :, :], src_ps[:, 0:NC * Q].rearrange(by_q, q=Q))
            dve.tensor_scalar(dst_idx[:, :, :], dst_ps[:, 0:NC * Q].rearrange(by_q, q=Q), float(N - 1), None, ALU.min)
            own(dve.tensor_copy(dst_pad[:, :, :], dst_ps[:, 0:NC * Q].rearrange(by_q, q=Q)))
            dve.tensor_scalar(bin_a_i[:, :, :], dst_pad[:, :, :], 9, 2, ALU.logical_shift_right, ALU.logical_shift_left)
            dve.tensor_scalar(bin_q_i[:, :, :], dst_pad[:, :, :], 3, None, ALU.bitwise_and)
            own(dve.tensor_scalar(bin_b_i[:, :, :], dst_pad[:, :, :], 2, P - 1, ALU.logical_shift_right, ALU.bitwise_and))
            dve.tensor_copy(bin_b[:, :, :], bin_b_i[:, :, :])
            own(dve.tensor_tensor(bin_a[:, :, :], bin_a_i[:, :, :], bin_q_i[:, :, :], ALU.add))
            for c in range(SLOTS):
                dve.tensor_copy(stage[:, c, 0:Q], src_idx[:, c, :])
                dve.tensor_copy(stage[:, c, Q:2 * Q], dst_idx[:, c, :]).then_inc(s_staged, 1)
            dve.wait_ge(s_weights, 16 * 12)

            def dst_columns(c, slot, parts):
                dve.wait_ge(s_turned, c + 1)
                if later(c, 2):
                    dve.wait_ge(s_hid_mm, c - 1)
                dve.tensor_copy(dst_T[:, slot % 2, :], dst_ps[:, :]).then_inc(s_dst_T, 1)
                if not isinstance(c, int) or c + SLOTS < NC:
                    dve.tensor_copy(stage[:, slot, 0:Q], src_idx[:, bass.ds(c + SLOTS, 1), :].rearrange("p a q -> p (a q)"))
                    dve.tensor_copy(stage[:, slot, Q:2 * Q], dst_idx[:, bass.ds(c + SLOTS, 1), :].rearrange("p a q -> p (a q)")).then_inc(s_staged, 1)

            def one_hots(c, slot, parts):
                if later(c, 2):
                    dve.wait_ge(s_hot_used, c - 1)
                for q in range(Q):
                    dve.tensor_scalar(hot_a[:, slot % 2, q, :], count[:, :], bin_a[:, bass.ds(c, 1), q], None, ALU.is_equal)
                    last = dve.tensor_scalar(hot_b[:, slot % 2, q, :], count[:, 0:P], bin_b[:, bass.ds(c, 1), q], None, ALU.is_equal)
                last.then_inc(s_hot, 1)

            def run_maximum(c, slot, parts):
                two = slot % 2
                dve.wait_ge(s_msg_mm, c + 1)
                dve.wait_ge(s_restart_in[two], landed(c, slot, 2))
                if later(c, 2):
                    dve.wait_ge(s_max_turned, c - 1)
                if later(c, 1):
                    dve.wait_ge(s_max, c)
                dve.tensor_tensor_scan(
                    max_T[:, two, :], restart[:, two, :], msg_ps[:, :],
                    max_T[:, 1 - two, CH - 1:CH] if later(c, 1) else RESTART, ALU.add, ALU.max).then_inc(s_max, 1)

            def message_rows(c, slot, parts):
                dve.wait_ge(s_max_turned, c + 1)
                if later(c, 2):
                    dve.wait_ge(s_rows_out[slot % 2], landed(c - 2, slot, 2))
                dve.tensor_tensor(max_rows[:, slot % 2, :, :], row_ps[:, :].rearrange("p (q f) -> p q f", q=Q),
                                  b2_bc[:, :, :], ALU.add).then_inc(s_rows, 1)

            pipeline(dve, [(0, dst_columns), (2, message_rows), (0, one_hots), (1, run_maximum)])

            dve.wait_ge(s_hot_used, NC + 1)
            own(dve.tensor_copy(hist[:, :, :], hist_ps[:, 0:NC * Q].rearrange("p (c q) -> p c q", q=Q)))
            dve.tensor_reduce(hist_p[:, :], hist[:, :, :], AX.X, ALU.add).then_inc(s_hist, 1)
            dve.wait_ge(s_prefix, 1)
            own(dve.tensor_copy(total[:, :], tot_ps[:, 0:NC]))
            own(dve.tensor_tensor_scan(total_scan[:, :], total[:, :], zeros[:, 0:NC], 0.0, ALU.add, ALU.add))
            own(dve.tensor_tensor(base[:, :], total_scan[:, :], total[:, :], ALU.subtract))
            own(dve.tensor_tensor(base[:, :], base[:, :], row_ps[:, 0:NC], ALU.add))
            own(dve.tensor_tensor(ends[:, :, 0], base[:, :], hist[:, :, 0], ALU.add))
            for q in range(1, Q):
                own(dve.tensor_tensor(ends[:, :, q], ends[:, :, q - 1], hist[:, :, q], ALU.add))
            own(dve.tensor_scalar(ends_off[:, :, :], ends[:, :, :], neg_zero_row[:, 0:1], None, ALU.add))
            own(dve.scalar_tensor_tensor(out=ends_sel[:, :, :], in0=hist[:, :, :], scalar=1.0, in1=ends_off[:, :, :],
                                         op0=ALU.min, op1=ALU.mult))
            own(dve.tensor_scalar(end_idx[:, :, :], ends_sel[:, :, :], zero_row[:, 0:1], None, ALU.add))
            for c in range(SLOTS):
                dve.tensor_copy(stage[:, c, 0:Q], end_idx[:, c, :]).then_inc(s_nstaged, 1)

            def agg_columns(c, slot, parts):
                qp = "f (q p) -> f q p"
                dve.wait_ge(s_nturned, c + 1)
                if later(c, 2):
                    dve.wait_ge(s_upd_mm, c - 1)
                dve.tensor_copy(dst_T[:, slot % 2, :].rearrange(qp, q=Q)[:, :, 0:parts],
                                dst_ps[:, :].rearrange(qp, q=Q)[:, :, 0:parts]).then_inc(s_agg_T, 1)
                if not isinstance(c, int) or c + SLOTS < NC:
                    dve.tensor_copy(stage[:, slot, 0:Q], end_idx[:, bass.ds(c + SLOTS, 1), :].rearrange("p a q -> p (a q)")).then_inc(s_nstaged, 1)

            def residual(c, slot, parts):
                two = slot % 2
                dve.wait_ge(s_y_mm, c + 1)
                if later(c, 2):
                    dve.wait_ge(s_out_ready, c - 1)
                dve.tensor_tensor(sum_rows[0:parts, two, :, :], x_rows[0:parts, slot, :, :],
                                  msg_ps[0:parts, :].rearrange("p (q f) -> p q f", q=Q), ALU.add).then_inc(s_sum, 1)
                dve.wait_ge(s_sum, c + 1)
                for q in range(Q):
                    last = dve.bn_stats(stats[0:parts, two, q, :], sum_rows[0:parts, two, q, :])
                last.then_inc(s_moments, 1)
                dve.wait_ge(s_moments, c + 1)
                dve.nop(nofuse=True)
                for q in range(Q):
                    last = dve.bn_aggr(mean_var[0:parts, two, q, :], stats[0:parts, two, q, :])
                last.then_inc(s_stat, 1)

            def normalise(c, slot, parts):
                two = slot % 2
                dve.wait_ge(s_std, c + 1)
                dve.reciprocal(rstd[0:parts, two, :], std[0:parts, two, :]).then_inc(s_rstd, 1)
                dve.wait_ge(s_rstd, c + 1)
                if later(c, 2):
                    dve.wait_ge(s_out[two], landed(c - 2, slot, 2))
                for q in range(Q):
                    last = dve.tensor_scalar(out_rows[0:parts, two, q, :], sum_rows[0:parts, two, q, :],
                                             mean_var[0:parts, two, q, 0:1], rstd[0:parts, two, q:q + 1],
                                             ALU.subtract, ALU.mult)
                last.then_inc(s_out_ready, 1)

            pipeline(dve, [(0, agg_columns), (3, normalise), (2, residual)], tail=TAILP)

        @block.tensor
        def _(pe):
            pe.wait_ge(s_const, 1)
            pe.wait_ge(s_lists_f, 1)
            for tile, turned in ((src_f, src_ps), (dst_f, dst_ps)):
                by_q = tile[:, :].rearrange("c (p q) -> c q p", q=Q)
                for q in range(Q):
                    last = pe.transpose(turned[:, q * NC:(q + 1) * NC], by_q[:, q, :], ident[0:NC, 0:NC])
            last.then_inc(s_lists_T, 1)
            pe.wait_ge(s_weights, 16 * 12)
            pe.wait_ge(s_moved, 16 * 6)
            pe.matmul(hist_ps[:, 0:NC * Q], zeros_b[:, 0:P], zeros_b[:, 0:NC * Q], start=True, stop=False)

            def turn_rows(c, slot, parts):
                pe.wait_ge(s_src_in[slot], landed(c, slot, SLOTS, Q))
                if isinstance(c, int) and c == 0:
                    pe.wait_ge(s_staged, 1)
                if later(c, 1):
                    pe.wait_ge(s_src_T, c)
                for q in range(Q):
                    pe.transpose(src_ps[:, q * P:(q + 1) * P], src_rows[:, slot, q, :], ident[:, :])
                pe.wait_ge(s_dst_in[slot], landed(c, slot, SLOTS, Q))
                if later(c, 1):
                    pe.wait_ge(s_dst_T, c)
                for q in range(Q):
                    last = pe.transpose(dst_ps[:, q * P:(q + 1) * P], dst_rows[:, slot, q, :], ident[:, :])
                last.then_inc(s_turned, 1)

            def histogram(c, slot, parts):
                pe.wait_ge(s_hot, c + 1)
                for q in range(Q):
                    last = pe.matmul(hist_ps[:, 0:NC * Q], hot_b[:, slot % 2, q, :], hot_a[:, slot % 2, q, :], start=False, stop=False)
                last.then_inc(s_hot_used, 1)

            def layer_1(c, slot, parts):
                two = slot % 2
                if later(c, 1):
                    pe.wait_ge(s_hid, c)
                pe.wait_ge(s_w_in[two], landed(c, slot, 2))
                pe.matmul(hid_ps[:, :], w1c9[:, :], w9[:, two, :].rearrange("r (p q) -> r q p", q=Q), start=True, stop=False)
                pe.wait_ge(s_src_T, c + 1)
                pe.matmul(hid_ps[:, :], w1a[:, :], src_T[:, two, :], start=False, stop=False)
                pe.wait_ge(s_dst_T, c + 1)
                pe.matmul(hid_ps[:, :], w1b[:, :], dst_T[:, two, :], start=False, stop=True).then_inc(s_hid_mm, 1)

            def layer_2(c, slot, parts):
                pe.wait_ge(s_hid, c + 1)
                if later(c, 1):
                    pe.wait_ge(s_max, c)
                pe.matmul(msg_ps[:, :], w2[:, :], hid_T[:, slot % 2, :].rearrange("f (q p) -> f p q", q=Q),
                          start=True, stop=True).then_inc(s_msg_mm, 1)

            def turn_maxima(c, slot, parts):
                pe.wait_ge(s_max, c + 1)
                if later(c, 1):
                    pe.wait_ge(s_rows, c)
                by_q = max_T[:, slot % 2, :].rearrange("f (p q) -> f q p", q=Q)
                for q in range(Q):
                    last = pe.transpose(row_ps[:, q * D:(q + 1) * D], by_q[:, q, :], ident[:, :])
                last.then_inc(s_max_turned, 1)

            pipeline(pe, [(0, turn_rows), (2, turn_maxima), (1, layer_1), (0, histogram), (1, layer_2)])

            pe.matmul(hist_ps[:, 0:NC * Q], zeros_b[:, 0:P], zeros_b[:, 0:NC * Q], start=False, stop=True).then_inc(s_hot_used, 1)
            pe.wait_ge(s_hist, 1)
            pe.wait_ge(s_rows, NC)
            pe.matmul(row_ps[:, 0:NC], before[:, :], hist_p[:, :], start=True, stop=True)
            pe.matmul(tot_ps[:, 0:NC], ones[:, :], hist_p[:, :], start=True, stop=True).then_inc(s_prefix, 1)

            def turn_node_rows(c, slot, parts):
                pe.wait_ge(s_x_in[slot], landed(c, slot, SLOTS))
                pe.wait_ge(s_x_T, c) if later(c, 1) else pe.wait_ge(s_src_T, NC)
                for q in range(Q):
                    pe.transpose(src_ps[:, q * P:q * P + parts], x_rows[0:parts, slot, q, :], ident[0:parts, 0:parts])
                pe.wait_ge(s_agg_in[slot], landed(c, slot, SLOTS, Q))
                pe.wait_ge(s_agg_T, c) if later(c, 1) else pe.wait_ge(s_dst_T, NC)
                for q in range(Q):
                    last = pe.transpose(dst_ps[:, q * P:q * P + parts], src_rows[0:parts, slot, q, :], ident[0:parts, 0:parts])
                last.then_inc(s_nturned, 1)

            def update_1(c, slot, parts):
                two = slot % 2
                pe.wait_ge(s_upd, c) if later(c, 1) else pe.wait_ge(s_hid, NC)
                pe.wait_ge(s_x_T, c + 1)
                pe.matmul(hid_ps[:, :], u1a[:, :], src_T[:, two, :], start=True, stop=False)
                pe.wait_ge(s_agg_T, c + 1)
                pe.matmul(hid_ps[:, :], u1b[:, :], dst_T[:, two, :], start=False, stop=True).then_inc(s_upd_mm, 1)

            def update_2(c, slot, parts):
                pe.wait_ge(s_sum, c) if later(c, 1) else pe.wait_ge(s_max, NC)
                pe.wait_ge(s_upd, c + 1)
                for q in range(Q):
                    pe.matmul(msg_ps[:, q * D:(q + 1) * D], ones_b[:, :], c2_3[:, 0:D], start=True, stop=False)
                    last = pe.matmul(msg_ps[:, q * D:(q + 1) * D], hid_T[:, slot % 2, q * P:(q + 1) * P], u2[:, :],
                                     start=False, stop=True)
                last.then_inc(s_y_mm, 1)

            pipeline(pe, [(0, turn_node_rows), (2, update_2), (1, update_1)], tail=TAILP)


_INS = ['x', 'src', 'dst', 'edge_weight', 'L0_gnn_W1', 'L0_gnn_b1', 'L0_gnn_W2', 'L0_gnn_b2',
        'L0_gnn_U1', 'L0_gnn_c1', 'L0_gnn_U2', 'L0_gnn_c2']


def kernel(**inputs):
    import numpy as _np
    import concourse.bacc as _bacc
    from concourse import mybir as _mybir
    from concourse.bass_utils import run_bass_kernel_spmd as _run

    nc = _bacc.Bacc("TRN2", target_bir_lowering=False, num_devices=1)
    arrays, args = {}, []
    for name in _INS:
        a = _np.ascontiguousarray(inputs[name])
        arrays[f"in_{name}_dram"] = a
        args.append(nc.dram_tensor(f"in_{name}_dram", a.shape, _mybir.dt.from_np(a.dtype), kind="ExternalInput").ap())
    x = inputs['x']
    out = nc.dram_tensor("out_0_dram", tuple(x.shape), _mybir.dt.float32, kind="ExternalOutput").ap()
    gnn_layer(nc, *args, out)
    r = _run(nc, [arrays], core_ids=[0])
    return r.results[0]["out_0_dram"]
```

```python
import concourse.bass as bass
from concourse import mybir
from contextlib import ExitStack


def gnn_layer(nc, x, src, dst, edge_weight, W1, b1, W2, b2, U1, c1, U2, c2, out):
    F32, F32R, BF16, F16 = mybir.dt.float32, mybir.dt.float32r, mybir.dt.bfloat16, mybir.dt.float16
    I32, U32 = mybir.dt.int32, mybir.dt.uint32
    ALU, ACT, AX = mybir.AluOpType, mybir.ActivationFunctionType, mybir.AxisListType

    N, D = x.shape
    E = src.shape[0]
    P = 128
    Q = 4
    CH = P * Q
    NC = -(-E // CH)
    assert N == E and D == P and NC % 2 == 0 and NC <= P
    EP = NC * CH
    TAIL = E - (NC - 1) * CH
    TAILP = TAIL // Q
    assert TAIL % Q == 0 and EP > N
    PAD_NODE = EP - 1
    RESTART = -3.0e38
    EPS = 1e-5
    GR = CH // 2
    WIN = 3 * P
    LAST_WIN = N - WIN
    LAST_EWIN = EP - WIN
    DE = D + 4
    NONE = -1.0e6
    NT = -(-N // P)
    PAIRS = 8
    SLOTS = 4

    w_rows = nc.dram_tensor("w_rows", (NC, 9, CH), BF16, kind="Internal").ap()
    restart_rows = nc.dram_tensor("restart_rows", (NC, CH), BF16, kind="Internal").ap()
    place_rows = nc.dram_tensor("place_rows", (NC, CH), F16, kind="Internal").ap()
    dst_rows = nc.dram_tensor("dst_rows", (NC, CH), F32, kind="Internal").ap()
    msg_rows = nc.dram_tensor("msg_rows", (EP, DE), F32, kind="Internal").ap()

    with ExitStack() as ctx:
        def sb(name, shape, dt):
            return ctx.enter_context(nc.sbuf_tensor(name, shape, dt))

        def ps(name):
            return ctx.enter_context(nc.psum_tensor(name, [P, CH], F32))

        def sem(name):
            return ctx.enter_context(nc.semaphore(name))

        ident = sb("ident", [P, P], F32)
        ones = sb("ones", [P, P], F32)
        ones_b = sb("ones_b", [3, P], BF16)
        count_i = sb("count_i", [P, CH], I32)
        count = sb("count", [P, CH], F16)
        eps = sb("eps", [P, 1], F32)
        w1a, w1b = sb("w1a", [P, D], F32), sb("w1b", [P, D], F32)
        w2 = sb("w2", [P, D], F32)
        u1a, u1b = sb("u1a", [P, D], F32), sb("u1b", [P, D], F32)
        u2 = sb("u2", [P, D], F32)
        w1a_hi, w1a_lo = sb("w1a_hi", [P, D], F32R), sb("w1a_lo", [P, D], F32R)
        w1b_hi, w1b_lo = sb("w1b_hi", [P, D], F32R), sb("w1b_lo", [P, D], F32R)
        w2_hi, w2_lo = sb("w2_hi", [P, D], F32R), sb("w2_lo", [P, D], F32R)
        u1b_hi, u1b_lo = sb("u1b_hi", [P, D], F32R), sb("u1b_lo", [P, D], F32R)
        b1_col, b2_col, c1_col = sb("b1_col", [P, 1], F32), sb("b2_col", [P, 1], F32), sb("c1_col", [P, 1], F32)
        w1c_f = sb("w1c_f", [3, 2, D], F32)
        w1c_part = sb("w1c_part", [3, 3, D], BF16)
        w1c12 = sb("w1c12", [12, D], BF16)
        bias_f = sb("bias_f", [3, 2, 2 * D], F32)
        bias_part = sb("bias_part", [3, 3, 2 * D], BF16)
        c2_3 = sb("c2_3", [3, D], BF16)

        src_i, dst_i, prev_i, next_i = (sb(n, [NC, CH], I32) for n in ("src_i", "dst_i", "prev_i", "next_i"))
        src_f, dst_f = sb("src_f", [NC, CH], F32), sb("dst_f", [NC, CH], F32)
        w_f = sb("w_f", [NC, 3, CH], F32)
        w_part = sb("w_part", [NC, 3, CH], BF16)
        restart_f = sb("restart_f", [NC, CH], F32)
        restart_b = sb("restart_b", [NC, CH], BF16)
        place_h = sb("place_h", [NC, CH], F16)
        ends_f = sb("ends_f", [NC, 3, CH], F32)
        src_idx = sb("src_idx", [P, NC, Q], I32)
        end_node = sb("end_node", [P, NC, Q], F32)
        bound_i, bound = sb("bound_i", [NC, 3], I32), sb("bound", [NC, 3], F32)
        last_sq, last_row = sb("last_sq", [NC, NC], F32), sb("last_row", [NC, NC], F32)
        below, found = sb("below", [NC, 3, CH], F32), sb("found", [NC, 3, CH], F32)
        far_i = found[:, 0, :].bitcast(I32)
        row_count, row_f, row_i = sb("row_count", [NC, 3], F32), sb("row_f", [NC, 3], F32), sb("row_i", [NC, 3], I32)
        in_row, start = sb("in_row", [NC, 3], F32), sb("start", [NC, 3], F32)
        node_base_i, node_base = sb("node_base_i", [P, NC], I32), sb("node_base", [P, NC], F32)

        stage = sb("stage", [P, SLOTS, Q], I32)
        src_rows = sb("src_rows", [P, SLOTS, Q, D], F32)
        src_hi, src_lo = sb("src_hi", [P, 2, CH], F32R), sb("src_lo", [P, 2, CH], F32R)
        dst_hi, dst_lo = sb("dst_hi", [P, 2, CH], F32R), sb("dst_lo", [P, 2, CH], F32R)
        w12 = sb("w12", [12, SLOTS, CH], BF16)
        restart, place = sb("restart", [P, SLOTS, CH], BF16), sb("place", [P, SLOTS, CH], F16)
        window = sb("window", [P, SLOTS, 2, 3, D], F32)
        window_hi, window_lo = sb("window_hi", [P, 2, 2, 3, D], F32R), sb("window_lo", [P, 2, 2, 3, D], F32R)
        pick = sb("pick", [P, 2, 3, CH], F32R)
        win_base_f = sb("win_base_f", [NC, 2], F32)
        ewin_base_f = sb("ewin_base_f", [NC, 2], F32)
        bases = sb("bases", [1, 4 * NC], I32)
        win_row_i = sb("win_row_i", [P, 3], I32)
        win_row = sb("win_row", [P, 3], F32)
        hid_hi, hid_lo = sb("hid_hi", [P, 2, CH], F32R), sb("hid_lo", [P, 2, CH], F32R)
        hid_T = sb("hid_T", [P, 2, CH], F32)
        max_T = sb("max_T", [P, 2, CH], F32)
        max_rows = sb("max_rows", [P, 2, Q, DE], F32)
        misfits = sb("misfits", [NC, 1], F32)
        any_misfit = sb("any_misfit", [1, 1], I32)
        tile_src, tile_dst = sb("tile_src", [P, 1], I32), sb("tile_dst", [P, 1], I32)
        tile_dst_row, tile_w = sb("tile_dst_row", [P, P], I32), sb("tile_w", [1, P], F32)
        w1c_row = sb("w1c_row", [1, D], F32)
        ewindow = sb("ewindow", [P, SLOTS, 2, 3, DE], F32)
        ewin_node = sb("ewin_node", [P, 2, 2, 3], F32)
        x_T = sb("x_T", [P, 2, CH], F32)
        msg_T = x_T
        x_rows = sb("x_rows", [P, SLOTS, Q, D], F32)
        sum_rows = sb("sum_rows", [P, SLOTS, Q, D], F32)
        out_rows = sb("out_rows", [P, 2, Q, D], F32)
        stats = sb("stats", [P, SLOTS, Q, 6], F32)
        mean_var = sb("mean_var", [P, SLOTS, Q, 2], F32)
        shift = sb("shift", [P, SLOTS, Q], F32)
        std, rstd = sb("std", [P, SLOTS, Q], F32), sb("rstd", [P, SLOTS, Q], F32)

        src_ps, hi_ps, hid_ps, msg_ps = ps("src_ps"), ps("hi_ps"), ps("hid_ps"), ps("msg_ps")
        row_ps, lo_ps, small_ps = ps("row_ps"), ps("lo_ps"), ps("small_ps")

        s_const, s_fill, s_lists, s_weights, s_small = (sem(n) for n in ("s_const", "s_fill", "s_lists", "s_weights", "s_small"))
        s_dve = sem("s_dve")
        s_split, s_moved = sem("s_split"), sem("s_moved")
        s_lists_f = sem("s_lists_f")
        s_src_in = [sem(f"s_src_in{k}") for k in range(SLOTS)]
        s_w_in, s_restart_in = [sem(f"s_w_in{k}") for k in range(SLOTS)], [sem(f"s_restart_in{k}") for k in range(SLOTS)]
        s_place_in = [sem(f"s_place_in{k}") for k in range(SLOTS)]
        s_window_in = [sem(f"s_window_in{k}") for k in range(SLOTS)]
        s_base_T, s_base, s_hi, s_lo, s_pick, s_picked = (sem(n) for n in ("s_base_T", "s_base", "s_hi", "s_lo", "s_pick", "s_picked"))
        s_rows_out = [sem(f"s_rows_out{k}") for k in range(2)]
        s_staged, s_turned, s_src_T, s_dst_T = sem("s_staged"), sem("s_turned"), sem("s_src_T"), sem("s_dst_T")
        s_hid_mm, s_hid, s_msg_mm, s_max, s_max_turned, s_rows = (sem(n) for n in ("s_hid_mm", "s_hid", "s_msg_mm", "s_max", "s_max_turned", "s_rows"))
        s_src_lo, s_last, s_last_T, s_found_idx, s_found = (sem(n) for n in ("s_src_lo", "s_last", "s_last_T", "s_found_idx", "s_found"))
        s_msg, s_column, s_t_msg = sem("s_msg"), sem("s_column"), sem("s_t_msg")
        s_hid_hi = sem("s_hid_hi")
        s_t_column = sem("s_t_column")
        s_normal, s_enode, s_recip = sem("s_normal"), sem("s_enode"), sem("s_recip")
        s_ehi, s_elo, s_epick, s_epicked = (sem(n) for n in ("s_ehi", "s_elo", "s_epick", "s_epicked"))
        s_ewindow_in, s_x_in = [sem(f"s_ewindow_in{k}") for k in range(SLOTS)], [sem(f"s_x_in{k}") for k in range(SLOTS)]
        s_out = [sem(f"s_out{k}") for k in range(2)]
        s_nturned, s_x_T, s_agg_T = sem("s_nturned"), sem("s_x_T"), sem("s_agg_T")
        s_upd_mm, s_upd, s_y_mm, s_sum, s_moments, s_stat, s_std, s_rstd, s_out_ready = (
            sem(n) for n in ("s_upd_mm", "s_upd", "s_y_mm", "s_sum", "s_moments", "s_stat", "s_std", "s_rstd", "s_out_ready"))

        s_padded, s_dst_lists, s_src_f, s_restart, s_place_stored, s_w_stored, s_ebase_T, s_ebase, s_src_turned, s_ends_T, s_src_idx, s_ends_read = (
            sem(n) for n in ("s_padded", "s_dst_lists", "s_src_f", "s_restart", "s_place_stored", "s_w_stored", "s_ebase_T", "s_ebase",
                             "s_src_turned", "s_ends_T", "s_src_idx", "s_ends_read"))
        s_dst_rows, s_start, s_ends, s_parts = sem("s_dst_rows"), sem("s_start"), sem("s_ends"), sem("s_parts")

        s_misfits, s_misfit_sum, s_misfit = sem("s_misfits"), sem("s_misfit_sum"), sem("s_misfit")
        s_blank, s_cleared, s_t_loaded, s_t_gathered, s_t_turned, s_t_columns, s_t_hid_mm, s_t_hid, s_t_msg_mm = (
            sem(n) for n in ("s_blank", "s_cleared", "s_t_loaded", "s_t_gathered", "s_t_turned", "s_t_columns", "s_t_hid_mm", "s_t_hid", "s_t_msg_mm"))
        s_t_dve, s_t_max, s_t_max_turned, s_t_rows, s_t_merged = (
            sem(n) for n in ("s_t_dve", "s_t_max", "s_t_max_turned", "s_t_rows", "s_t_merged"))
        s_n_loaded, s_n_agg, s_n_turned, s_n_columns, s_n_upd_mm, s_n_upd, s_n_y_mm, s_n_var, s_n_std, s_n_ready, s_n_out, s_n_dve = (
            sem(n) for n in ("s_n_loaded", "s_n_agg", "s_n_turned", "s_n_columns", "s_n_upd_mm", "s_n_upd", "s_n_y_mm", "s_n_var",
                             "s_n_std", "s_n_ready", "s_n_out", "s_n_dve"))

        t_src_rows, t_dst_rows, t_held = src_rows[:, 0, 0, :], src_rows[:, 0, 1, :], ewindow[:, 0, 0, 0, :]
        t_a_T, t_b_T, t_hid_T, t_msg_T, t_max_T = x_T[:, 0, 0:P], x_T[:, 1, 0:P], hid_T[:, 0, 0:P], hid_T[:, 1, 0:P], max_T[:, 0, 0:P]
        t_rows = max_rows[:, 0, 0, :]
        t_pairs = window[:, 0:2, :, :, :].rearrange("p s g k f -> p (s g k f)")[:, 0:PAIRS * P].rearrange("p (j i) -> p j i", i=P)

        block = ctx.enter_context(nc.Block())

        def pipeline(eng, stages, tail=P):
            depth = max(lag for lag, _ in stages)
            head = SLOTS * (-(-(depth + SLOTS) // SLOTS))
            rest = head + (NC - SLOTS - head) // SLOTS * SLOTS

            def turn(t, turn_slot):
                for lag, step in stages:
                    c = t - lag
                    if isinstance(t, int) and not 0 <= c < NC:
                        continue
                    step(c, (turn_slot - lag) % SLOTS, tail if isinstance(c, int) and c == NC - 1 else P)

            for t in range(head):
                turn(t, t % SLOTS)
            with eng.Fori(head, rest - SLOTS + 1, SLOTS) as t:
                for k in range(SLOTS):
                    turn(t + k, k)
            for t in range(rest, NC + depth):
                turn(t, t % SLOTS)

        def tiles(eng, step):
            step(0, 0)
            with eng.Fori(1, NT - 1) as t:
                step(t, t * P)
            step(NT - 1, N - P)

        def choose(eng, general, windowed):
            eng.wait_ge(s_misfit, 1)
            with eng.If(eng.value_load(any_misfit[0:1, 0:1], min_val=0, max_val=1) > 0):
                general()
            with eng.Else():
                windowed()
            eng.end_ifs()

        def later(c, lag):
            return not isinstance(c, int) or c >= lag

        def landed(c, slot, slots, per=1):
            return ((c - slot % slots) // slots + 1) * 16 * per

        @block.gpsimd
        def _(pool):
            pool.iota(dst_i[:, :], pattern=[[0, CH]], base=PAD_NODE, channel_multiplier=0)
            pool.iota(prev_i[:, :], pattern=[[0, CH]], base=PAD_NODE, channel_multiplier=0)
            pool.iota(far_i, pattern=[[0, CH]], base=2 * EP, channel_multiplier=0)
            pool.iota(src_i[:, :], pattern=[[0, CH]], base=0, channel_multiplier=0)
            pool.iota(next_i[:, :], pattern=[[0, CH]], base=PAD_NODE, channel_multiplier=0)
            pool.memset(w_f[:, 0, :], 0.0).then_inc(s_padded, 1)
            pool.memset(ident[:, :], 0.0)
            pool.memset(ones[:, :], 1.0)
            pool.memset(ones_b[:, :], 1.0)
            pool.memset(eps[:, :], EPS)
            pool.memset(w12[:, :, :], 1.0)
            pool.iota(count_i[:, :], pattern=[[1, CH]], base=0, channel_multiplier=0)
            pool.iota(bound_i[:, :], pattern=[[GR, 3]], base=0, channel_multiplier=CH)
            pool.iota(node_base_i[:, :], pattern=[[CH, NC]], base=0, channel_multiplier=0)
            pool.memset(max_rows[:, :, :, :], 0.0)
            pool.iota(win_row_i[:, :], pattern=[[P, 3]], base=0, channel_multiplier=1).then_inc(s_fill, 1)
            pool.wait_ge(s_fill, 1)
            pool.affine_select(out=ident[:, :], in_=ident[:, :], pattern=[[-1, P]], compare_op=ALU.not_equal,
                               fill=1.0, base=0, channel_multiplier=1).then_inc(s_const, 1)
            pool.wait_ge(s_found_idx, 1)
            pool.wait_ge(s_dst_rows, 16)
            for k in range(3):
                pool.indirect_dma_start(out=found[:, k, :], out_offset=None, in_=dst_rows[:, :],
                                        in_offset=bass.IndirectOffsetOnAxis(ap=row_i[:, k:k + 1].bitcast(U32), axis=0)).then_inc(s_found, 16)

            def windowed():
                def gather(c, slot, parts):
                    pool.wait_ge(s_staged, c + 1)
                    if later(c, SLOTS):
                        pool.nop(nofuse=True)
                        pool.wait_ge(s_turned, c - SLOTS + 1)
                    pool.nop(nofuse=True)
                    for q in range(Q):
                        pool.indirect_dma_start(
                            out=src_rows[:, slot, q, :], out_offset=None, in_=x[:, :],
                            in_offset=bass.IndirectOffsetOnAxis(ap=stage[:, slot, q:q + 1].bitcast(U32), axis=0),
                        ).then_inc(s_src_in[slot], 16)

                pipeline(pool, [(0, gather)])

                def ewindow_rest(c, slot, parts):
                    pool.wait_ge(s_ehi, c + 1)
                    if later(c, 2):
                        pool.nop(nofuse=True)
                        pool.wait_ge(s_epicked, c - 1)
                    pool.nop(nofuse=True)
                    pool.tensor_tensor(window_lo[:, slot % 2, :, :, :], ewindow[:, slot, :, :, 0:D],
                                       window_hi[:, slot % 2, :, :, :].bitcast(F32), ALU.subtract).then_inc(s_elo, 1)

                pipeline(pool, [(0, ewindow_rest)], tail=TAILP)

            def general():
                pool.memset(max_rows[:, 0, :, 0:D], RESTART).then_inc(s_blank, 1)

                def merge_edges(t, first):
                    pool.wait_ge(s_t_loaded, 64 * (t + 1))
                    pool.nop(nofuse=True)
                    for rows, idx, table in ((t_src_rows, tile_src, x), (t_dst_rows, tile_dst, x), (t_held, tile_dst, msg_rows)):
                        pool.indirect_dma_start(out=rows, out_offset=None, in_=table[:, :],
                                                in_offset=bass.IndirectOffsetOnAxis(ap=idx[:, 0:1].bitcast(U32), axis=0)).then_inc(s_t_gathered, 16)
                    pool.wait_ge(s_t_rows, t + 1)
                    pool.nop(nofuse=True)
                    pool.indirect_dma_start(out=msg_rows[:, :], out_offset=bass.IndirectOffsetOnAxis(ap=tile_dst[:, 0:1].bitcast(U32), axis=0),
                                            in_=t_rows, in_offset=None).then_inc(s_t_merged, 16)

                tiles(pool, merge_edges)

            choose(pool, general, windowed)

        @block.sync
        def _(sp):
            sp.wait_ge(s_padded, 1)
            full = (NC - 1) * CH

            def row_of(lst, first, end):
                return lst[first:end].rearrange("(c j) -> c j", c=1)

            def rows_of(lst, first, end):
                return lst[first:end].rearrange("(c j) -> c j", j=CH)

            sp.dma_start(dst_i[0:NC - 1, :], rows_of(dst, 0, full)).then_inc(s_dst_lists, 16)
            sp.dma_start(dst_i[NC - 1:NC, 0:TAIL], row_of(dst, full, E)).then_inc(s_dst_lists, 16)
            sp.dma_start(prev_i[0:1, 0:1], row_of(dst, 0, 1)).then_inc(s_dst_lists, 16)
            sp.dma_start(prev_i[0:1, 1:CH], row_of(dst, 0, CH - 1)).then_inc(s_dst_lists, 16)
            sp.dma_start(prev_i[1:NC - 1, :], rows_of(dst, CH - 1, full - 1)).then_inc(s_dst_lists, 16)
            sp.dma_start(prev_i[NC - 1:NC, 0:TAIL], row_of(dst, full - 1, E - 1)).then_inc(s_dst_lists, 16)
            far_full = (NC - 2) * CH
            sp.dma_start(far_i[0:NC - 2, :], rows_of(dst, WIN, far_full + WIN)).then_inc(s_dst_lists, 16)
            sp.dma_start(far_i[NC - 2:NC - 1, 0:E - WIN - far_full], row_of(dst, far_full + WIN, E)).then_inc(s_dst_lists, 16)
            sp.dma_start(src_i[0:NC - 1, :], rows_of(src, 0, full)).then_inc(s_lists, 16)
            sp.dma_start(src_i[NC - 1:NC, 0:TAIL], row_of(src, full, E)).then_inc(s_lists, 16)
            sp.dma_start(w_f[0:NC - 1, 0, :], rows_of(edge_weight, 0, full)).then_inc(s_lists, 16)
            sp.dma_start(w_f[NC - 1:NC, 0, 0:TAIL], row_of(edge_weight, full, E)).then_inc(s_lists, 16)
            sp.dma_start(next_i[0:NC - 1, :], rows_of(dst, 1, full + 1)).then_inc(s_lists, 16)
            sp.dma_start(next_i[NC - 1:NC, 0:TAIL - 1], row_of(dst, full + 1, E)).then_inc(s_lists, 16)
            sp.wait_ge(s_lists_f, 1)
            sp.dma_start(dst_rows, dst_f[:, :]).then_inc(s_dst_rows, 16)
            sp.wait_ge(s_restart, 1)
            sp.dma_start(place_rows, place_h[:, :]).then_inc(s_place_stored, 16)
            sp.dma_start(restart_rows, restart_b[:, :]).then_inc(s_place_stored, 16)
            sp.wait_ge(s_place_stored, 16 * 2)
            sp.wait_ge(s_base, 1)

            def windowed():
                def load(c, slot, parts):
                    if later(c, SLOTS):
                        sp.wait_ge(s_lo, c - SLOTS + 1)
                    for g in range(2):
                        first = sp.value_load(bases[0:1, bass.ds(c + g * NC, 1)], min_val=0, max_val=LAST_WIN)
                        sp.dma_start(window[:, slot, g, :, :], x[bass.ds(first, WIN), :].rearrange("(k p) f -> p k f", p=P)).then_inc(s_window_in[slot], 16)
                    sp.dma_start(place[:, slot, :], place_rows[bass.ds(c, 1), :].to_broadcast([P, CH])).then_inc(s_place_in[slot], 16)

                def load_weights(c, slot, parts):
                    if not later(c, 1):
                        sp.wait_ge(s_fill, 1)
                        sp.wait_ge(s_w_stored, 16 * 3)
                    if later(c, SLOTS):
                        sp.wait_ge(s_hid_mm, c - SLOTS + 1)
                    sp.dma_start(w12[0:9, slot, :], w_rows[bass.ds(c, 1), :, :].rearrange("a r j -> (a r) j")).then_inc(s_w_in[slot], 16)

                def load_restarts(c, slot, parts):
                    if later(c, SLOTS):
                        sp.wait_ge(s_max, c - SLOTS + 1)
                    sp.dma_start(restart[:, slot, :], restart_rows[bass.ds(c, 1), :].to_broadcast([P, CH])).then_inc(s_restart_in[slot], 16)

                pipeline(sp, [(0, load), (1, load_weights), (2, load_restarts)])

                for two in range(2):
                    sp.wait_ge(s_rows_out[two], 16 * (NC // 2))
                sp.wait_ge(s_ebase, 1)

                def load_messages(c, slot, parts):
                    if later(c, SLOTS):
                        sp.wait_ge(s_elo, c - SLOTS + 1)
                        sp.wait_ge(s_enode, c - SLOTS + 1)
                    for g in range(2):
                        first = sp.value_load(bases[0:1, bass.ds(c + (2 + g) * NC, 1)], min_val=0, max_val=LAST_EWIN)
                        sp.dma_start(ewindow[:, slot, g, :, :], msg_rows[bass.ds(first, WIN), :].rearrange("(k p) f -> p k f", p=P)).then_inc(s_ewindow_in[slot], 16)

                def load_x(c, slot, parts):
                    if later(c, SLOTS):
                        sp.wait_ge(s_sum, c - SLOTS + 1)
                    sp.dma_start(x_rows[0:parts, slot, :, :].rearrange("p q f -> p (q f)"),
                                 x[bass.ds(c * CH, parts * Q), :].rearrange("(p q) f -> p (q f)", q=Q)).then_inc(s_x_in[slot], 16)

                def store_out(c, slot, parts):
                    sp.wait_ge(s_normal, c + 1)
                    sp.wait_ge(s_out_ready, c + 1)
                    sp.dma_start(out[bass.ds(c * CH, parts * Q), :].rearrange("(p q) f -> p (q f)", q=Q),
                                 out_rows[0:parts, slot % 2, :, :].rearrange("p q f -> p (q f)")).then_inc(s_out[slot % 2], 16)

                pipeline(sp, [(0, load_messages), (0, load_x), (8, store_out)], tail=TAILP)
                for two in range(2):
                    sp.wait_ge(s_out[two], 16 * (NC // 2))

            def general():
                sp.wait_ge(s_w_stored, 16 * 3)
                sp.wait_ge(s_found, 16 * 3)
                sp.wait_ge(s_blank, 1)
                with sp.Fori(0, NC) as c:
                    sp.dma_start(msg_rows[bass.ds(c * CH, CH), :].rearrange("(p q) f -> p (q f)", q=Q),
                                 max_rows[:, 0, :, :].rearrange("p q f -> p (q f)")).then_inc(s_cleared, 16)
                sp.dma_start(w1c_row[:, :], W1[2 * D:2 * D + 1, :]).then_inc(s_cleared, 16)
                sp.wait_ge(s_cleared, 16 * (NC + 1))

                def load_edges(t, first):
                    if later(t, 1):
                        sp.wait_ge(s_t_merged, 16 * t)
                    sp.dma_start(tile_src[:, :], src[bass.ds(first, P)].rearrange("(p a) -> p a", a=1)).then_inc(s_t_loaded, 16)
                    sp.dma_start(tile_dst[:, :], dst[bass.ds(first, P)].rearrange("(p a) -> p a", a=1)).then_inc(s_t_loaded, 16)
                    sp.dma_start(tile_dst_row[:, :], dst[bass.ds(first, P)].rearrange("(a p) -> a p", a=1).to_broadcast([P, P])).then_inc(s_t_loaded, 16)
                    sp.dma_start(tile_w[:, :], edge_weight[bass.ds(first, P)].rearrange("(a p) -> a p", a=1)).then_inc(s_t_loaded, 16)

                tiles(sp, load_edges)
                sp.wait_ge(s_t_merged, 16 * NT)

                def nodes(t, first):
                    if later(t, 1):
                        sp.wait_ge(s_n_out, 16 * t)
                    sp.dma_start(t_src_rows, x[bass.ds(first, P), :]).then_inc(s_n_loaded, 16)
                    sp.dma_start(t_held, msg_rows[bass.ds(first, P), :]).then_inc(s_n_loaded, 16)
                    sp.wait_ge(s_n_ready, t + 1)
                    sp.dma_start(out[bass.ds(first, P), :], out_rows[:, 0, 0, :]).then_inc(s_n_out, 16)

                tiles(sp, nodes)
                sp.wait_ge(s_n_out, 16 * NT)

            choose(sp, general, windowed)

        @block.scalar
        def _(act):
            act.dma_start(bias_f[:, 0, 0:D], c2.rearrange("(a f) -> a f", a=1).to_broadcast([3, D])).then_inc(s_small, 16)
            act.dma_start(bias_f[:, 0, D:2 * D], b1.rearrange("(a f) -> a f", a=1).to_broadcast([3, D])).then_inc(s_small, 16)
            act.dma_start(w1c_f[:, 0, :], W1[2 * D:2 * D + 1, :].to_broadcast([3, D])).then_inc(s_small, 16)
            for tile, part in ((w1a, W1[0:D, :]), (w1b, W1[D:2 * D, :]), (w2, W2[:, :]),
                               (u1a, U1[0:D, :]), (u1b, U1[D:2 * D, :]), (u2, U2[:, :])):
                act.dma_start(tile[:, :], part).then_inc(s_weights, 16)
            for tile, bias in ((b1_col, b1), (b2_col, b2), (c1_col, c1)):
                act.dma_start(tile[:, :], bias.rearrange("(p a) -> p a", a=1)).then_inc(s_weights, 16)
            act.wait_ge(s_split, 1)
            act.wait_ge(s_dst_lists, 16 * 8)
            for k in range(3):
                act.dma_start(w1c12[3 * k:3 * k + 3, :], w1c_part[:, k, :]).then_inc(s_moved, 16)
                act.dma_start(c2_3[k:k + 1, :], bias_part[0:1, k, 0:D]).then_inc(s_moved, 16)
                act.dma_start(w1c12[9 + k:10 + k, :], bias_part[0:1, k, D:2 * D]).then_inc(s_moved, 16)
            act.wait_ge(s_split, 2)
            for k in range(3):
                act.dma_start(w_rows[:, 3 * k:3 * k + 3, :], w_part[:, :, :]).then_inc(s_w_stored, 16)
            act.wait_ge(s_weights, 16 * 9)

            def windowed():
                def split_window(c, slot, parts):
                    act.wait_ge(s_window_in[slot], landed(c, slot, SLOTS, 2))
                    if later(c, 2):
                        act.wait_ge(s_picked, c - 1)
                    act.activation(window_hi[:, slot % 2, :, :, :].rearrange("p g k f -> p (g k f)"),
                                   window[:, slot, :, :, :].rearrange("p g k f -> p (g k f)"), ACT.Copy).then_inc(s_hi, 1)

                def src_columns(c, slot, parts):
                    act.wait_ge(s_turned, c + 1)
                    if later(c, 2):
                        act.wait_ge(s_hid_mm, c - 1)
                    act.activation(src_hi[:, slot % 2, :], src_ps[:, :], ACT.Copy).then_inc(s_src_T, 1)

                def dst_columns(c, slot, parts):
                    act.wait_ge(s_picked, c + 1)
                    if later(c, 2):
                        act.wait_ge(s_hid_mm, c - 1)
                    act.activation(dst_hi[:, slot % 2, :], hi_ps[:, :], ACT.Copy)
                    act.activation(dst_lo[:, slot % 2, :], lo_ps[:, :], ACT.Copy).then_inc(s_dst_T, 1)

                def hidden(c, slot, parts):
                    act.wait_ge(s_hid_mm, c + 1)
                    if later(c, 2):
                        act.wait_ge(s_msg_mm, c - 1)
                    act.activation(hid_hi[:, slot % 2, :], hid_ps[:, :], ACT.Relu).then_inc(s_hid_hi, 1)

                def messages(c, slot, parts):
                    act.wait_ge(s_msg_mm, c + 1)
                    if later(c, 2):
                        act.wait_ge(s_max, c - 1)
                    act.activation(msg_T[:, slot % 2, :], msg_ps[:, :], ACT.Identity, bias=b2_col[:, 0:1]).then_inc(s_msg, 1)

                def message_rows(c, slot, parts):
                    act.wait_ge(s_max_turned, c + 1)
                    if later(c, 2):
                        act.wait_ge(s_rows_out[slot % 2], landed(c - 2, slot, 2))
                    act.activation(max_rows[:, slot % 2, :, 0:D], row_ps[:, :].rearrange("p (q f) -> p q f", q=Q), ACT.Copy).then_inc(s_rows, 1)

                def store(c, slot, parts):
                    act.wait_ge(s_rows, c + 1)
                    act.wait_ge(s_column, c + 1)
                    act.dma_start(msg_rows[bass.ds(c * CH, CH), :].rearrange("(p q) f -> p (q f)", q=Q),
                                 max_rows[:, slot % 2, :, :].rearrange("p q f -> p (q f)")).then_inc(s_rows_out[slot % 2], 16)

                pipeline(act, [(4, messages), (1, src_columns), (2, hidden), (0, split_window), (1, dst_columns), (5, message_rows), (6, store)])

                def split_ewindow(c, slot, parts):
                    act.wait_ge(s_ewindow_in[slot], landed(c, slot, SLOTS, 2))
                    if later(c, 2):
                        act.wait_ge(s_epicked, c - 1)
                    act.activation(window_hi[:, slot % 2, :, :, :], ewindow[:, slot, :, :, 0:D], ACT.Copy).then_inc(s_ehi, 1)

                def x_columns(c, slot, parts):
                    act.wait_ge(s_nturned, c + 1)
                    if later(c, 2):
                        act.wait_ge(s_upd_mm, c - 1)
                    act.activation(x_T[:, slot % 2, :].rearrange("f (p q) -> f q p", q=Q)[:, :, 0:parts],
                                   src_ps[:, :].rearrange("f (q p) -> f q p", q=Q)[:, :, 0:parts], ACT.Copy).then_inc(s_x_T, 1)

                def agg_columns(c, slot, parts):
                    act.wait_ge(s_epicked, c + 1)
                    if later(c, 2):
                        act.wait_ge(s_upd_mm, c - 1)
                    act.activation(dst_hi[:, slot % 2, :], hi_ps[:, :], ACT.Copy)
                    act.activation(dst_lo[:, slot % 2, :], lo_ps[:, :], ACT.Copy).then_inc(s_agg_T, 1)

                def update_hidden(c, slot, parts):
                    act.wait_ge(s_upd_mm, c + 1)
                    if later(c, 2):
                        act.wait_ge(s_y_mm, c - 1)
                    act.activation(hid_T[:, slot % 2, :], hid_ps[:, :], ACT.Relu, bias=c1_col[:, 0:1]).then_inc(s_upd, 1)

                def deviation(c, slot, parts):
                    act.wait_ge(s_stat, c + 1)
                    act.activation(std[0:parts, slot, :], mean_var[0:parts, slot, :, 1], ACT.Sqrt,
                                   bias=eps[0:parts, 0:1]).then_inc(s_std, 1)

                def normalise(c, slot, parts):
                    two = slot % 2
                    act.wait_ge(s_rstd, c + 1)
                    if later(c, 2):
                        act.wait_ge(s_out[two], landed(c - 2, slot, 2))
                    for q in range(Q - 1):
                        last = act.activation(out_rows[0:parts, two, q, :], sum_rows[0:parts, slot, q, :], ACT.Identity,
                                              bias=shift[0:parts, slot, q:q + 1], scale=rstd[0:parts, slot, q:q + 1])
                    last.then_inc(s_normal, 1)

                pipeline(act, [(0, split_ewindow), (6, normalise), (1, x_columns), (4, deviation), (2, update_hidden), (1, agg_columns)], tail=TAILP)

            def general():
                def edge_columns(t, first):
                    act.wait_ge(s_t_turned, t + 1)
                    act.activation(t_a_T, src_ps[:, 0:P], ACT.Copy)
                    act.activation(t_b_T, hi_ps[:, 0:P], ACT.Copy).then_inc(s_t_columns, 1)
                    act.wait_ge(s_t_hid_mm, t + 1)
                    act.activation(t_hid_T, hid_ps[:, 0:P], ACT.Relu, bias=b1_col[:, 0:1]).then_inc(s_t_hid, 1)
                    act.wait_ge(s_t_msg_mm, t + 1)
                    act.activation(t_msg_T, msg_ps[:, 0:P], ACT.Identity, bias=b2_col[:, 0:1]).then_inc(s_t_msg, 1)

                tiles(act, edge_columns)

                def node_columns(t, first):
                    act.wait_ge(s_n_turned, t + 1)
                    act.activation(t_a_T, src_ps[:, 0:P], ACT.Copy)
                    act.activation(t_b_T, hi_ps[:, 0:P], ACT.Copy).then_inc(s_n_columns, 1)
                    act.wait_ge(s_n_upd_mm, t + 1)
                    act.activation(t_hid_T, hid_ps[:, 0:P], ACT.Relu, bias=c1_col[:, 0:1]).then_inc(s_n_upd, 1)
                    act.wait_ge(s_n_var, t + 1)
                    act.activation(std[:, 0, 0:1], mean_var[:, 0, 0, 1:2], ACT.Sqrt, bias=eps[:, 0:1]).then_inc(s_n_std, 1)

                tiles(act, node_columns)

            choose(act, general, windowed)

        @block.vector
        def _(dve):
            steps = [0]

            def own(ins):
                steps[0] += 1
                ins.then_inc(s_dve, 1)
                dve.wait_ge(s_dve, steps[0])

            def split(part, value, rest):
                own(dve.tensor_copy(part(0), value))
                own(dve.tensor_tensor(rest, value, part(0), ALU.subtract))
                own(dve.tensor_copy(part(1), rest))
                own(dve.tensor_tensor(value, rest, part(1), ALU.subtract))
                return dve.tensor_copy(part(2), value)

            dve.wait_ge(s_small, 16 * 3)
            split(lambda k: bias_part[:, k, :], bias_f[:, 0, :], bias_f[:, 1, :])
            split(lambda k: w1c_part[:, k, :], w1c_f[:, 0, :], w1c_f[:, 1, :]).then_inc(s_split, 1)
            dve.wait_ge(s_dst_lists, 16 * 8)
            dve.tensor_copy(dst_f[:, :], dst_i[:, :]).then_inc(s_lists_f, 1)
            dve.wait_ge(s_lists_f, 1)
            own(dve.tensor_scalar(win_base_f[:, :], dst_f[:, :].rearrange("c (g j) -> c g j", g=2)[:, :, 0], float(LAST_WIN), None, ALU.min))
            for g in range(2):
                last = dve.tensor_scalar(place_h[:, g * GR:(g + 1) * GR], dst_f[:, g * GR:(g + 1) * GR],
                                         win_base_f[:, g:g + 1], None, ALU.subtract)
            own(last)
            dve.tensor_tensor(ends_f[:, 0, :], dst_i[:, :], prev_i[:, :], ALU.is_lt)
            dve.tensor_scalar(ends_f[:, 2, :], place_h[:, :], float(WIN - 1), None, ALU.is_gt)
            own(dve.tensor_tensor(ends_f[:, 1, :], far_i, dst_i[:, :], ALU.subtract))
            own(dve.tensor_scalar(ends_f[:, 1, :], ends_f[:, 1, :], float(GR), None, ALU.is_lt))
            dve.tensor_reduce(misfits[:, 0:1], ends_f[:, :, :].rearrange("c k j -> c (k j)"), AX.X, ALU.add).then_inc(s_misfits, 1)
            own(dve.tensor_tensor(restart_f[:, :], dst_i[:, :], prev_i[:, :], ALU.not_equal))
            dve.tensor_scalar(restart_b[:, :], restart_f[:, :], RESTART, None, ALU.mult).then_inc(s_restart, 1)
            dve.wait_ge(s_const, 1)
            dve.tensor_copy(bound[:, :], bound_i[:, :])
            dve.tensor_scalar(last_sq[:, :], ones[0:NC, 0:NC], dst_f[:, CH - 1:CH], None, ALU.mult).then_inc(s_last, 1)
            dve.wait_ge(s_misfit_sum, 1)
            dve.tensor_scalar(any_misfit[:, :], msg_ps[0:1, 0:1], float(EP - E), None, ALU.is_gt).then_inc(s_misfit, 1)
            dve.wait_ge(s_base_T, 1)
            dve.tensor_copy(bases[:, 0:2 * NC], row_ps[0:1, 0:2 * NC]).then_inc(s_base, 1)
            dve.wait_ge(s_lists, 16 * 6)
            dve.tensor_copy(src_f[:, :], src_i[:, :]).then_inc(s_src_f, 1)
            dve.wait_ge(s_last_T, 1)
            own(dve.tensor_copy(last_row[:, :], small_ps[0:NC, 0:NC]))
            for k in range(3):
                last = dve.tensor_scalar(below[:, k, 0:NC], last_row[:, :], bound[:, k:k + 1], None, ALU.is_lt)
            own(last)
            own(dve.tensor_reduce(row_count[:, :], below[:, :, 0:NC], AX.X, ALU.add))
            own(dve.tensor_scalar(row_f[:, :], row_count[:, :], float(NC - 1), None, ALU.min))
            dve.tensor_copy(row_i[:, :], row_f[:, :]).then_inc(s_found_idx, 1)
            by_q = "p (q c) -> p c q"
            dve.wait_ge(s_src_turned, 1)
            dve.tensor_copy(src_idx[:, :, :], src_ps[:, 0:NC * Q].rearrange(by_q, q=Q)).then_inc(s_src_idx, 1)
            dve.wait_ge(s_src_idx, 1)
            for c in range(SLOTS):
                dve.tensor_copy(stage[:, c, 0:Q], src_idx[:, c, :]).then_inc(s_staged, 1)
            split(lambda k: w_part[:, k, :], w_f[:, 0, :], w_f[:, 1, :]).then_inc(s_split, 1)
            own(dve.tensor_tensor(ends_f[:, 0, :], dst_i[:, :], next_i[:, :], ALU.is_equal))
            dve.scalar_tensor_tensor(out=ends_f[:, 1, :], in0=ends_f[:, 0, :], scalar=NONE, in1=dst_f[:, :],
                                     op0=ALU.mult, op1=ALU.add).then_inc(s_ends, 1)
            dve.wait_ge(s_weights, 16 * 9)
            for whole, hi, lo in ((w1a, w1a_hi, w1a_lo), (w1b, w1b_hi, w1b_lo), (w2, w2_hi, w2_lo), (u1b, u1b_hi, u1b_lo)):
                own(dve.tensor_copy(hi[:, :], whole[:, :]))
                dve.tensor_tensor(lo[:, :], whole[:, :], hi[:, :].bitcast(F32), ALU.subtract).then_inc(s_parts, 1)
            dve.tensor_copy(count[:, :], count_i[:, :])
            dve.tensor_copy(node_base[:, :], node_base_i[:, :])
            dve.tensor_copy(win_row[:, :], win_row_i[:, :])
            dve.wait_ge(s_ends_T, 1)
            dve.tensor_copy(end_node[:, :, :], hi_ps[:, 0:NC * Q].rearrange(by_q, q=Q)).then_inc(s_ends_read, 1)
            dve.wait_ge(s_ends_read, 1)
            def windowed():
                def src_rest(c, slot, parts):
                    dve.wait_ge(s_src_T, c + 1)
                    if later(c, 2):
                        dve.wait_ge(s_hid_mm, c - 1)
                    dve.tensor_tensor(src_lo[:, slot % 2, :], src_ps[:, :], src_hi[:, slot % 2, :].bitcast(F32), ALU.subtract).then_inc(s_src_lo, 1)

                def hidden_rest(c, slot, parts):
                    dve.wait_ge(s_hid_hi, c + 1)
                    if later(c, 2):
                        dve.wait_ge(s_msg_mm, c - 1)
                    dve.scalar_tensor_tensor(out=hid_lo[:, slot % 2, :], in0=hid_ps[:, :], scalar=0.0, in1=hid_hi[:, slot % 2, :].bitcast(F32),
                                             op0=ALU.max, op1=ALU.subtract).then_inc(s_hid, 1)

                def next_indices(c, slot, parts):
                    if not isinstance(c, int) or c + SLOTS < NC:
                        dve.wait_ge(s_src_in[slot], landed(c, slot, SLOTS, Q))
                        dve.tensor_copy(stage[:, slot, 0:Q], src_idx[:, bass.ds(c + SLOTS, 1), :].rearrange("p a q -> p (a q)")).then_inc(s_staged, 1)

                def pick_columns(c, slot, parts):
                    two = slot % 2
                    dve.wait_ge(s_place_in[slot], landed(c, slot, SLOTS))
                    if later(c, 2):
                        dve.wait_ge(s_picked, c - 1)
                    for k in range(3):
                        last = dve.tensor_scalar(pick[:, two, k, :], place[:, slot, :], win_row[:, k:k + 1], None, ALU.is_equal)
                    last.then_inc(s_pick, 1)
                    dve.wait_ge(s_hi, c + 1)
                    flat = "p g k f -> p (g k f)"
                    dve.tensor_tensor(window_lo[:, two, :, :, :].rearrange(flat), window[:, slot, :, :, :].rearrange(flat),
                                      window_hi[:, two, :, :, :].rearrange(flat).bitcast(F32), ALU.subtract).then_inc(s_lo, 1)

                def run_maximum(c, slot, parts):
                    two = slot % 2
                    dve.wait_ge(s_msg, c + 1)
                    dve.wait_ge(s_restart_in[slot], landed(c, slot, SLOTS))
                    if later(c, 2):
                        dve.wait_ge(s_max_turned, c - 1)
                    if later(c, 1):
                        dve.wait_ge(s_max, c)
                    dve.tensor_tensor_scan(
                        max_T[:, two, :], restart[:, slot, :], msg_T[:, two, :],
                        max_T[:, 1 - two, CH - 1:CH] if later(c, 1) else RESTART, ALU.add, ALU.max).then_inc(s_max, 1)

                def node_column(c, slot, parts):
                    if later(c, 2):
                        dve.wait_ge(s_rows_out[slot % 2], landed(c - 2, slot, 2))
                    dve.tensor_copy(max_rows[:, slot % 2, :, D], end_node[:, bass.ds(c, 1), :].rearrange("p a q -> p (a q)")).then_inc(s_column, 1)

                pipeline(dve, [(0, next_indices), (4, run_maximum), (1, src_rest), (2, hidden_rest), (0, pick_columns), (5, node_column)])

                dve.wait_ge(s_found, 16 * 3)
                for k in range(3):
                    last = dve.tensor_scalar(below[:, k, :], found[:, k, :], bound[:, k:k + 1], None, ALU.is_lt)
                own(last)
                own(dve.tensor_reduce(in_row[:, :], below[:, :, :], AX.X, ALU.add))
                own(dve.scalar_tensor_tensor(out=start[:, :], in0=row_f[:, :], scalar=float(CH), in1=in_row[:, :],
                                             op0=ALU.mult, op1=ALU.add))
                dve.tensor_scalar(ewin_base_f[:, :], start[:, 0:2], float(LAST_EWIN), None, ALU.min).then_inc(s_start, 1)
                dve.wait_ge(s_ebase_T, 1)
                dve.tensor_copy(bases[:, 2 * NC:4 * NC], small_ps[0:1, 0:2 * NC]).then_inc(s_ebase, 1)

                def end_nodes(c, slot, parts):
                    dve.wait_ge(s_ewindow_in[slot], landed(c, slot, SLOTS, 2))
                    if later(c, 2):
                        dve.wait_ge(s_epick, c - 1)
                    dve.tensor_scalar(ewin_node[:, slot % 2, :, :], ewindow[:, slot, :, :, D], node_base[:, bass.ds(c, 1)], None,
                                      ALU.subtract).then_inc(s_enode, 1)

                def pick_ends(c, slot, parts):
                    two = slot % 2
                    dve.wait_ge(s_enode, c + 1)
                    if later(c, 2):
                        dve.wait_ge(s_epicked, c - 1)
                    for g in range(2):
                        for k in range(3):
                            last = dve.tensor_scalar(pick[:, two, k, g * GR:(g + 1) * GR], count[:, g * GR:(g + 1) * GR],
                                                     ewin_node[:, two, g, k:k + 1], None, ALU.is_equal)
                    last.then_inc(s_epick, 1)

                def residual(c, slot, parts):
                    dve.wait_ge(s_y_mm, c + 1)
                    if later(c, SLOTS):
                        dve.wait_ge(s_normal, c - SLOTS + 1)
                        dve.wait_ge(s_out_ready, c - SLOTS + 1)
                    dve.tensor_tensor(sum_rows[0:parts, slot, :, :], x_rows[0:parts, slot, :, :],
                                      (msg_ps, row_ps)[slot % 2][0:parts, :].rearrange("p (q f) -> p q f", q=Q), ALU.add).then_inc(s_sum, 1)

                def statistics(c, slot, parts):
                    dve.wait_ge(s_sum, c + 1)
                    for q in range(Q):
                        last = dve.bn_stats(stats[0:parts, slot, q, :], sum_rows[0:parts, slot, q, :])
                    last.then_inc(s_moments, 1)

                def moments(c, slot, parts):
                    dve.wait_ge(s_moments, c + 1)
                    dve.nop(nofuse=True)
                    for q in range(Q):
                        last = dve.bn_aggr(mean_var[0:parts, slot, q, :], stats[0:parts, slot, q, :])
                    last.then_inc(s_stat, 1)

                def factors(c, slot, parts):
                    dve.wait_ge(s_std, c + 1)
                    dve.reciprocal(rstd[0:parts, slot, :], std[0:parts, slot, :]).then_inc(s_recip, 1)

                def shifts(c, slot, parts):
                    dve.wait_ge(s_recip, c + 1)
                    dve.scalar_tensor_tensor(out=shift[0:parts, slot, :], in0=mean_var[0:parts, slot, :, 0], scalar=-1.0,
                                             in1=rstd[0:parts, slot, :], op0=ALU.mult, op1=ALU.mult).then_inc(s_rstd, 1)

                def normalise(c, slot, parts):
                    q = Q - 1
                    dve.wait_ge(s_rstd, c + 1)
                    if later(c, 2):
                        dve.wait_ge(s_out[slot % 2], landed(c - 2, slot, 2))
                    dve.tensor_scalar(out_rows[0:parts, slot % 2, q, :], sum_rows[0:parts, slot, q, :],
                                      mean_var[0:parts, slot, q, 0:1], rstd[0:parts, slot, q:q + 1],
                                      ALU.subtract, ALU.mult).then_inc(s_out_ready, 1)

                pipeline(dve, [(3, residual), (0, end_nodes), (5, factors), (3, statistics), (5, shifts), (0, pick_ends), (3, moments), (6, normalise)], tail=TAILP)

            def general():
                per_tile = 3 * P // PAIRS - 1

                def merge(t, first):
                    done = [t * per_tile]

                    def own_step(ins):
                        done[0] = done[0] + 1
                        ins.then_inc(s_t_dve, 1)
                        dve.wait_ge(s_t_dve, done[0])

                    dve.wait_ge(s_t_msg, t + 1)
                    for j in range(0, P, PAIRS):
                        own_step(dve.tensor_tensor(t_pairs, tile_dst_row[:, j:j + PAIRS].unsqueeze(2).to_broadcast([P, PAIRS, P]),
                                                   tile_dst_row[:, :].unsqueeze(1).to_broadcast([P, PAIRS, P]), ALU.not_equal))
                        own_step(dve.scalar_tensor_tensor(out=t_pairs, in0=t_pairs, scalar=RESTART,
                                                          in1=t_msg_T.unsqueeze(1).to_broadcast([P, PAIRS, P]),
                                                          op0=ALU.mult, op1=ALU.add))
                        last = dve.tensor_reduce(t_max_T[:, j:j + PAIRS], t_pairs, AX.X, ALU.max)
                        if j + PAIRS < P:
                            own_step(last)
                    last.then_inc(s_t_max, 1)
                    dve.wait_ge(s_t_max_turned, t + 1)
                    dve.wait_ge(s_t_gathered, 48 * (t + 1))
                    dve.tensor_tensor(t_rows[:, 0:D], row_ps[:, 0:D], t_held[:, 0:D], ALU.max).then_inc(s_t_rows, 1)

                dve.wait_ge(s_cleared, 16 * (NC + 1))
                dve.tensor_scalar(t_rows[:, D:DE], ones[:, 0:DE - D], 1.0, None, ALU.mult).then_inc(s_t_column, 1)
                dve.wait_ge(s_t_column, 1)
                tiles(dve, merge)

                def update(t, first):
                    done = [t * 3]

                    def own_step(ins):
                        done[0] = done[0] + 1
                        ins.then_inc(s_n_dve, 1)
                        dve.wait_ge(s_n_dve, done[0])

                    dve.wait_ge(s_n_loaded, 32 * (t + 1))
                    dve.tensor_scalar(t_dst_rows, t_held[:, 0:D], t_held[:, D:D + 1], None, ALU.mult).then_inc(s_n_agg, 1)
                    dve.wait_ge(s_n_y_mm, t + 1)
                    own_step(dve.tensor_tensor(sum_rows[:, 0, 0, :], t_src_rows, msg_ps[:, 0:D], ALU.add))
                    own_step(dve.bn_stats(stats[:, 0, 0, :], sum_rows[:, 0, 0, :]))
                    dve.nop(nofuse=True)
                    dve.bn_aggr(mean_var[:, 0, 0, :], stats[:, 0, 0, :]).then_inc(s_n_var, 1)
                    dve.wait_ge(s_n_std, t + 1)
                    own_step(dve.reciprocal(rstd[:, 0, 0:1], std[:, 0, 0:1]))
                    dve.tensor_scalar(out_rows[:, 0, 0, :], sum_rows[:, 0, 0, :], mean_var[:, 0, 0, 0:1], rstd[:, 0, 0:1],
                                      ALU.subtract, ALU.mult).then_inc(s_n_ready, 1)

                tiles(dve, update)

            choose(dve, general, windowed)

        @block.tensor
        def _(pe):
            pe.wait_ge(s_const, 1)
            pe.wait_ge(s_misfits, 1)
            pe.matmul(msg_ps[0:1, 0:1], ones[0:NC, 0:1], misfits[:, :], start=True, stop=True).then_inc(s_misfit_sum, 1)
            for g in range(2):
                last = pe.transpose(row_ps[0:1, g * NC:(g + 1) * NC], win_base_f[:, g:g + 1], ident[0:NC, 0:NC])
            last.then_inc(s_base_T, 1)
            pe.wait_ge(s_last, 1)
            pe.matmul(small_ps[0:NC, 0:NC], last_sq[:, :], ident[0:NC, 0:NC], start=True, stop=True).then_inc(s_last_T, 1)
            pe.wait_ge(s_src_f, 1)
            for q in range(Q):
                last = pe.transpose(src_ps[:, q * NC:(q + 1) * NC], src_f[:, q * P:(q + 1) * P], ident[0:NC, 0:NC])
            last.then_inc(s_src_turned, 1)
            pe.wait_ge(s_ends, 1)
            ends_by_q = ends_f[:, 1, :].rearrange("c (p q) -> c q p", q=Q)
            for q in range(Q):
                last = pe.transpose(hi_ps[:, q * NC:(q + 1) * NC], ends_by_q[:, q, :], ident[0:NC, 0:NC])
            last.then_inc(s_ends_T, 1)
            pe.wait_ge(s_weights, 16 * 9)
            pe.wait_ge(s_moved, 16 * 9)
            pe.wait_ge(s_fill, 1)
            pe.wait_ge(s_parts, 4)
            pe.wait_ge(s_ends_read, 1)

            def windowed():
                def turn_rows(c, slot, parts):
                    pe.wait_ge(s_src_in[slot], landed(c, slot, SLOTS, Q))
                    if later(c, 1):
                        pe.wait_ge(s_src_lo, c)
                    for q in range(Q):
                        last = pe.transpose(src_ps[:, q * P:(q + 1) * P], src_rows[:, slot, q, :], ident[:, :])
                    last.then_inc(s_turned, 1)

                def pick_rows(c, slot, parts):
                    two = slot % 2
                    pe.wait_ge(s_pick, c + 1)
                    pe.wait_ge(s_lo, c + 1)
                    if later(c, 1):
                        pe.wait_ge(s_dst_T, c)
                    for g in range(2):
                        for k in range(3):
                            for part, bank in ((window_hi, hi_ps), (window_lo, lo_ps)):
                                last = pe.matmul(bank[:, g * GR:(g + 1) * GR], part[:, two, g, k, :], pick[:, two, k, g * GR:(g + 1) * GR],
                                                 start=(k == 0), stop=(k == 2))
                    last.then_inc(s_picked, 1)

                def product_3(bank, hi, lo, in_hi, in_lo, stop, start=False):
                    pe.matmul(bank, hi[:, :], in_hi, start=start, stop=False)
                    pe.matmul(bank, lo[:, :], in_hi, start=False, stop=False)
                    return pe.matmul(bank, hi[:, :], in_lo, start=False, stop=stop)

                def layer_1(c, slot, parts):
                    two = slot % 2
                    if later(c, 1):
                        pe.wait_ge(s_hid, c)
                    pe.wait_ge(s_w_in[slot], landed(c, slot, SLOTS))
                    pe.matmul(hid_ps[:, :], w1c12[:, :], w12[:, slot, :], start=True, stop=False)
                    pe.wait_ge(s_src_lo, c + 1)
                    product_3(hid_ps[:, :], w1a_hi, w1a_lo, src_hi[:, two, :], src_lo[:, two, :], False)
                    pe.wait_ge(s_dst_T, c + 1)
                    product_3(hid_ps[:, :], w1b_hi, w1b_lo, dst_hi[:, two, :], dst_lo[:, two, :], True).then_inc(s_hid_mm, 1)

                def layer_2(c, slot, parts):
                    pe.wait_ge(s_hid, c + 1)
                    if later(c, 1):
                        pe.wait_ge(s_msg, c)
                    product_3(msg_ps[:, :], w2_hi, w2_lo, hid_hi[:, slot % 2, :], hid_lo[:, slot % 2, :], True, start=True).then_inc(s_msg_mm, 1)

                def turn_maxima(c, slot, parts):
                    pe.wait_ge(s_max, c + 1)
                    if later(c, 1):
                        pe.wait_ge(s_rows, c)
                    by_q = max_T[:, slot % 2, :].rearrange("f (p q) -> f q p", q=Q)
                    for q in range(Q):
                        last = pe.transpose(row_ps[:, q * D:(q + 1) * D], by_q[:, q, :], ident[:, :])
                    last.then_inc(s_max_turned, 1)

                pipeline(pe, [(2, layer_1), (1, pick_rows), (5, turn_maxima), (3, layer_2), (0, turn_rows)])

                pe.wait_ge(s_start, 1)
                for g in range(2):
                    last = pe.transpose(small_ps[0:1, g * NC:(g + 1) * NC], ewin_base_f[:, g:g + 1], ident[0:NC, 0:NC])
                last.then_inc(s_ebase_T, 1)

                def turn_node_rows(c, slot, parts):
                    pe.wait_ge(s_x_in[slot], landed(c, slot, SLOTS))
                    pe.wait_ge(s_x_T, c) if later(c, 1) else pe.wait_ge(s_src_lo, NC)
                    for q in range(Q):
                        last = pe.transpose(src_ps[:, q * P:q * P + parts], x_rows[0:parts, slot, q, :], ident[0:parts, 0:parts])
                    last.then_inc(s_nturned, 1)

                def pick_ends(c, slot, parts):
                    two = slot % 2
                    pe.wait_ge(s_epick, c + 1)
                    pe.wait_ge(s_elo, c + 1)
                    pe.wait_ge(s_agg_T, c) if later(c, 1) else pe.wait_ge(s_dst_T, NC)
                    for g in range(2):
                        for k in range(3):
                            for part, bank in ((window_hi, hi_ps), (window_lo, lo_ps)):
                                last = pe.matmul(bank[:, g * GR:(g + 1) * GR], part[:, two, g, k, :], pick[:, two, k, g * GR:(g + 1) * GR],
                                                 start=(k == 0), stop=(k == 2))
                    last.then_inc(s_epicked, 1)

                def update_1(c, slot, parts):
                    two = slot % 2
                    pe.wait_ge(s_upd, c) if later(c, 1) else pe.wait_ge(s_hid, NC)
                    pe.wait_ge(s_x_T, c + 1)
                    pe.matmul(hid_ps[:, :], u1a[:, :], x_T[:, two, :], start=True, stop=False)
                    pe.wait_ge(s_agg_T, c + 1)
                    product_3(hid_ps[:, :], u1b_hi, u1b_lo, dst_hi[:, two, :], dst_lo[:, two, :], True).then_inc(s_upd_mm, 1)

                def update_2(c, slot, parts):
                    bank = (msg_ps, row_ps)[slot % 2]
                    if later(c, 2):
                        pe.wait_ge(s_sum, c - 1)
                    else:
                        pe.wait_ge(s_rows, NC)
                    pe.wait_ge(s_upd, c + 1)
                    by_q = hid_T[:, slot % 2, :].rearrange("f (p q) -> f q p", q=Q)
                    for q in range(Q):
                        pe.matmul(bank[:, q * D:(q + 1) * D], ones_b[:, :], c2_3[:, 0:D], start=True, stop=False)
                        last = pe.matmul(bank[:, q * D:(q + 1) * D], by_q[:, q, :], u2[:, :],
                                         start=False, stop=True)
                    last.then_inc(s_y_mm, 1)

                pipeline(pe, [(1, turn_node_rows), (2, update_1), (1, pick_ends), (2, update_2)], tail=TAILP)

            def general():
                def messages(t, first):
                    pe.wait_ge(s_t_gathered, 48 * (t + 1))
                    pe.transpose(src_ps[:, 0:P], t_src_rows, ident[:, :])
                    pe.transpose(hi_ps[:, 0:P], t_dst_rows, ident[:, :]).then_inc(s_t_turned, 1)
                    pe.wait_ge(s_t_columns, t + 1)
                    pe.matmul(hid_ps[:, 0:P], w1c_row[:, :], tile_w[:, :], start=True, stop=False)
                    pe.matmul(hid_ps[:, 0:P], w1a[:, :], t_a_T, start=False, stop=False)
                    pe.matmul(hid_ps[:, 0:P], w1b[:, :], t_b_T, start=False, stop=True).then_inc(s_t_hid_mm, 1)
                    pe.wait_ge(s_t_hid, t + 1)
                    pe.matmul(msg_ps[:, 0:P], w2[:, :], t_hid_T, start=True, stop=True).then_inc(s_t_msg_mm, 1)
                    pe.wait_ge(s_t_max, t + 1)
                    pe.transpose(row_ps[:, 0:D], t_max_T, ident[:, :]).then_inc(s_t_max_turned, 1)

                tiles(pe, messages)

                def update(t, first):
                    pe.wait_ge(s_n_agg, t + 1)
                    pe.transpose(src_ps[:, 0:P], t_src_rows, ident[:, :])
                    pe.transpose(hi_ps[:, 0:P], t_dst_rows, ident[:, :]).then_inc(s_n_turned, 1)
                    pe.wait_ge(s_n_columns, t + 1)
                    pe.matmul(hid_ps[:, 0:P], u1a[:, :], t_a_T, start=True, stop=False)
                    pe.matmul(hid_ps[:, 0:P], u1b[:, :], t_b_T, start=False, stop=True).then_inc(s_n_upd_mm, 1)
                    pe.wait_ge(s_n_upd, t + 1)
                    pe.matmul(msg_ps[:, 0:D], ones_b[:, :], c2_3[:, 0:D], start=True, stop=False)
                    pe.matmul(msg_ps[:, 0:D], t_hid_T, u2[:, :], start=False, stop=True).then_inc(s_n_y_mm, 1)

                tiles(pe, update)

            choose(pe, general, windowed)


_INS = ['x', 'src', 'dst', 'edge_weight', 'L0_gnn_W1', 'L0_gnn_b1', 'L0_gnn_W2', 'L0_gnn_b2',
        'L0_gnn_U1', 'L0_gnn_c1', 'L0_gnn_U2', 'L0_gnn_c2']


def kernel(**inputs):
    import numpy as _np
    import concourse.bacc as _bacc
    from concourse import mybir as _mybir
    from concourse.bass_utils import run_bass_kernel_spmd as _run

    nc = _bacc.Bacc("TRN2", target_bir_lowering=False, num_devices=1)
    arrays, args = {}, []
    for name in _INS:
        a = _np.ascontiguousarray(inputs[name])
        arrays[f"in_{name}_dram"] = a
        args.append(nc.dram_tensor(f"in_{name}_dram", a.shape, _mybir.dt.from_np(a.dtype), kind="ExternalInput").ap())
    x = inputs['x']
    out = nc.dram_tensor("out_0_dram", tuple(x.shape), _mybir.dt.float32, kind="ExternalOutput").ap()
    gnn_layer(nc, *args, out)
    r = _run(nc, [arrays], core_ids=[0])
    return r.results[0]["out_0_dram"]
```
